# Optimizing a Trainium2 kernel written in Bass

```python
import numpy as np
import jax
import jax.numpy as jnp

def _softmax(x, axis=-1):
    return jax.nn.softmax(x, axis=axis)

def _gelu(x):
    return jax.nn.gelu(x, approximate=True)

def _silu(x):
    return jax.nn.silu(x)

def _sigmoid(x):
    return jax.nn.sigmoid(x)

def _layernorm(x, axis=-1, eps=1e-05):
    m = jnp.mean(x, axis=axis, keepdims=True)
    v = jnp.var(x, axis=axis, keepdims=True)
    return (x - m) / jnp.sqrt(v + eps)

def _scatter_add(tgt, idx, src, axis=0):
    return tgt.at[idx].add(src)

def _segment_sum(src, seg, n):
    return jax.ops.segment_sum(src, seg, n)
kernel_name = 'mk_xattn_seq_d1_seqx_r4_954da3'

def setup_inputs(seed: int=0):
    np.random.seed(seed)
    _w = jnp.asarray

    def _rec_inputs():
        import jax
        import jax.numpy as jnp
        _rk = jax.random.key(seed)
        x = -0.0003929 + 0.9999 * jax.random.normal(jax.random.fold_in(_rk, 1), (16, 112, 1024), jnp.float32)
        _lenS = 112 - jax.random.randint(jax.random.fold_in(_rk, 7), (16,), 0, max(1, 112 // 4) + 1, jnp.int32)
        _lenS2 = 375 - jax.random.randint(jax.random.fold_in(_rk, 8), (16,), 0, max(1, 375 // 4) + 1, jnp.int32)
        _ctx_4096P = jax.random.normal(jax.random.fold_in(_rk, 11), (16, 16, 1024), jnp.float32)
        _ctx_4096c = jax.random.dirichlet(jax.random.fold_in(_rk, 511), 0.3 * jnp.ones((16,), jnp.float32), (16, 375))
        _ctx_4096t = jnp.einsum('bsk,bkd->bsd', _ctx_4096c, _ctx_4096P)
        _ctx_4096t = _ctx_4096t * jax.lax.rsqrt(jnp.mean(jnp.square(_ctx_4096t)) + 1e-12) * 0.953939
        ctx_4096 = 2.81802e-05 + 1.00001 * (_ctx_4096t + 0.3 * jax.random.normal(jax.random.fold_in(_rk, 611), (16, 375, 1024), jnp.float32))
        return (x, ctx_4096)
    x, ctx_4096 = _rec_inputs()

    def _L0_xattn_setup():
        import jax, jax.numpy as jnp
        import numpy as np
        H = 1024
        NH = 32
        NKV = 8
        HD = H // NH
        R = 16
        SCALING = 32.0 / 16.0

        def _lora_linear(x, W, A, B):
            return x @ W + SCALING * (x @ A @ B)
        key = jax.random.key(seed)
        ks = jax.random.split(key, 16)
        d = {'hidden_states': jax.random.normal(ks[0], (4, 256, H), jnp.float32), 'traces': jax.random.normal(ks[1], (4, 256, H), jnp.float32), 'Wq': jax.random.normal(ks[2], (H, H), jnp.float32) * 0.02, 'Aq': jax.random.normal(ks[3], (H, R), jnp.float32) * 0.02, 'Bq': jax.random.normal(ks[4], (R, H), jnp.float32) * 0.02, 'Wk': jax.random.normal(ks[5], (H, NKV * HD), jnp.float32) * 0.02, 'Ak': jax.random.normal(ks[6], (H, R), jnp.float32) * 0.02, 'Bk': jax.random.normal(ks[7], (R, NKV * HD), jnp.float32) * 0.02, 'Wv': jax.random.normal(ks[8], (H, NKV * HD), jnp.float32) * 0.02, 'Av': jax.random.normal(ks[9], (H, R), jnp.float32) * 0.02, 'Bv': jax.random.normal(ks[10], (R, NKV * HD), jnp.float32) * 0.02, 'Wo': jax.random.normal(ks[11], (H, H), jnp.float32) * 0.02, 'Ao': jax.random.normal(ks[12], (H, R), jnp.float32) * 0.02, 'Bo': jax.random.normal(ks[13], (R, H), jnp.float32) * 0.02}
        return d
    _L0_xattn_all = _L0_xattn_setup()
    _L0_xattn_in = {k: v for k, v in _L0_xattn_all.items() if k in ('Wq', 'Aq', 'Bq', 'Wk', 'Ak', 'Bk', 'Wv', 'Av', 'Bv', 'Wo', 'Ao', 'Bo')}
    del _L0_xattn_all
    return {'x': x, 'ctx_4096': ctx_4096, 'L0_xattn_Wq': _L0_xattn_in['Wq'], 'L0_xattn_Aq': _L0_xattn_in['Aq'], 'L0_xattn_Bq': _L0_xattn_in['Bq'], 'L0_xattn_Wk': _L0_xattn_in['Wk'], 'L0_xattn_Ak': _L0_xattn_in['Ak'], 'L0_xattn_Bk': _L0_xattn_in['Bk'], 'L0_xattn_Wv': _L0_xattn_in['Wv'], 'L0_xattn_Av': _L0_xattn_in['Av'], 'L0_xattn_Bv': _L0_xattn_in['Bv'], 'L0_xattn_Wo': _L0_xattn_in['Wo'], 'L0_xattn_Ao': _L0_xattn_in['Ao'], 'L0_xattn_Bo': _L0_xattn_in['Bo']}

def reference(x, ctx_4096, L0_xattn_Wq, L0_xattn_Aq, L0_xattn_Bq, L0_xattn_Wk, L0_xattn_Ak, L0_xattn_Bk, L0_xattn_Wv, L0_xattn_Av, L0_xattn_Bv, L0_xattn_Wo, L0_xattn_Ao, L0_xattn_Bo):
    import jax
    import jax.numpy as jnp

    def _L0_xattn_ref(hidden_states, traces, Wq, Aq, Bq, Wk, Ak, Bk, Wv, Av, Bv, Wo, Ao, Bo):
        import jax, jax.numpy as jnp
        import numpy as np
        H = 1024
        NH = 32
        NKV = 8
        HD = H // NH
        R = 16
        SCALING = 32.0 / 16.0

        def _lora_linear(x, W, A, B):
            return x @ W + SCALING * (x @ A @ B)
        bsz, q_len, _ = hidden_states.shape
        t_len = traces.shape[1]
        groups = NH // NKV
        q = _lora_linear(hidden_states, Wq, Aq, Bq).reshape(bsz, q_len, NH, HD)
        q = jnp.transpose(q, (0, 2, 1, 3))
        k = _lora_linear(traces, Wk, Ak, Bk).reshape(bsz, t_len, NKV, HD)
        v = _lora_linear(traces, Wv, Av, Bv).reshape(bsz, t_len, NKV, HD)
        k = jnp.transpose(k, (0, 2, 1, 3))
        v = jnp.transpose(v, (0, 2, 1, 3))
        k = jnp.repeat(k, groups, axis=1)
        v = jnp.repeat(v, groups, axis=1)
        scores = jnp.einsum('bhqd,bhtd->bhqt', q, k) / jnp.sqrt(jnp.asarray(HD, q.dtype))
        attn = jax.nn.softmax(scores, axis=-1)
        context = jnp.einsum('bhqt,bhtd->bhqd', attn, v)
        context = jnp.transpose(context, (0, 2, 1, 3)).reshape(bsz, q_len, H)
        out = _lora_linear(context, Wo, Ao, Bo)
        return hidden_states + out
    x = _L0_xattn_ref(x, ctx_4096, L0_xattn_Wq, L0_xattn_Aq, L0_xattn_Bq, L0_xattn_Wk, L0_xattn_Ak, L0_xattn_Bk, L0_xattn_Wv, L0_xattn_Av, L0_xattn_Bv, L0_xattn_Wo, L0_xattn_Ao, L0_xattn_Bo)
    return x

_drawn_inputs = setup_inputs


def setup_inputs(seed=0):
    import zlib

    import numpy as np

    out = dict(_drawn_inputs(seed))
    spreads = {}
    factors = {'L0_xattn_Aq': 8.0, 'L0_xattn_Bq': 8.0, 'L0_xattn_Ak': 8.0, 'L0_xattn_Bk': 8.0}
    for name, (base, spread) in spreads.items():
        noise = np.random.default_rng([zlib.crc32(name.encode()), seed]).standard_normal(out[name].shape)
        drawn = base * np.exp(spread * noise) if base else spread * noise
        out[name] = jnp.asarray(drawn.astype(out[name].dtype))
    for name, factor in factors.items():
        out[name] = (out[name] * factor).astype(out[name].dtype)
    return out
```

```python
from contextlib import ExitStack

import concourse.bass as bass
from concourse import mybir

ALU = mybir.AluOpType
ACT = mybir.ActivationFunctionType
AX = mybir.AxisListType
F32 = mybir.dt.float32
F32R = mybir.dt.float32r

B, NQ, H = 16, 112, 1024
NT = 375
NH, NKV, HD = 32, 8, 32
R = 16
LORA = 32.0 / 16.0
P = 128
KC = H // P
HALVES = 2
JH = NKV // HALVES
RH = NH // NKV
QH = RH * NQ
KVW = NKV * HD
TC = 3
TR = NT // TC
NTE = NT + 1
QG = 4
GROUPS = B // QG
SM = 1.0 / float(HD) ** 0.5
ROWS = B * NQ
OT = ROWS // P
BANK = 512
WBLK = H
assert TR * TC == NT and QH <= BANK and OT * P == ROWS and GROUPS * QG == B

STK = 3 * HD
NS = TC * JH
STM = STK + 1

NAT = 0
STB = 2
TURN = 3
VA, VB = 4, 5
CTX = 6
DEN = 7
FOLD = 2
FOLD_O = 4
DENSE = 4

PLAN = sorted(
    [("S", i, 0.02 + 0.075 * i) for i in range(TC * JH)]
    + [("P", 0, 0.46), ("P", 1, 0.66), ("P", 2, 0.94), ("D", 0, 0.14)]
    + [("R", 0, 0.17), ("R", 1, 0.21), ("R", 2, 0.29), ("R", 3, 0.33), ("A", 0, 0.40)]
    + [("N", i, t) for i, t in enumerate((0.03, 0.10, 0.25, 0.36, 0.50, 0.61, 0.72, 0.83))]
    + [("M", 0, 0.92)],
    key=lambda item: item[2])
LAG = 2
OLAG = 4


def half_order(h, has):
    dense = []
    if h == 0:
        for k in range(KC):
            dense += [("V", t, k) for t in range(TC) if "V" in has]
            dense += [("T", k - LAG, 0)] if "T" in has and k >= LAG else []
    if h == 1:
        for k in range(KC):
            dense += [("K", 0, k)] if "K" in has else []
            dense += [("T", KC - LAG + k // 2, 0)] if "T" in has and k % 2 == 0 and k // 2 < LAG else []
        dense += [("K", 1, k) for k in range(KC) if "K" in has]
    for name, first in (("W0", 0), ("W1", 4), ("W2", 8)):
        if name in has:
            for n in range(first, first + 4):
                dense += [("W", n, 0)] if n < KC else []
                dense += [("O", n - OLAG, 0)] if OLAG <= n < KC + OLAG else []
    plan = [item for item in PLAN if ("A" in has if item[0] in "SP" else "D" in has if item[0] in "DRA" else "N" in has)]
    order = []
    for n, piece in enumerate(dense):
        while plan and plan[0][2] * len(dense) <= n:
            order.append((plan[0][0], plan[0][1], 0))
            plan.pop(0)
        order.append(piece)
    order += [(kind, i, 0) for kind, i, _ in plan]
    return order + [("E", 0, 0)]


def at_least(eng, sem, n):
    if not isinstance(n, int) or n > 0:
        eng.wait_ge(sem, n)


def xattn_kernel(nc, x, ctxt, Wq, Aq, Bq, Wk, Ak, Bk, Wv, Av, Bv, Wo, Ao, Bo, out):
    stack = ExitStack()
    with stack:
        base = (nc.sbuf_base + 31) // 32 * 32
        limit = nc.sbuf_usable_end
        top = [base]

        def region(size):
            at = top[0]
            top[0] += (size + 31) // 32 * 32
            assert top[0] <= limit, (top[0], limit)
            return at

        def place(name, shape, dt, at):
            n = 4
            for s in shape[1:]:
                n *= s
            return nc.alloc_sbuf_tensor_at(name, shape, dt, offset=at), at + (n + 31) // 32 * 32

        r_small = region(512 + 128 + 128 + 2 * NQ * 4 + 512)
        r_ab = region(2 * 4 * H)
        r_w = region(2 * KC * H * 4)
        r_kv = region(4 * KC * KVW * 4)
        r_ct = region(2 * KC * QG * NQ * 4)
        r_cin = region(TC * H * 4)
        r_ks = region(2 * NKV * NTE * 4)
        r_v = region(2 * TC * KVW * 4)
        r_x = region(QG * H * 4 + 2 * QG * QH * 4)

        at = r_small
        ident, at = place("ident", [P, P], F32, at)
        ones, at = place("ones", [TR, HD], F32, at)
        maxima, at = place("maxima", [NQ, HALVES, JH * RH], F32, at)
        neg_max, at = place("neg_max", [JH * RH, HALVES, NQ], F32R, at)
        a_in, at = place("a_in", [P, KC, R], F32, at)
        a_dup, at = place("a_dup", [P, KC, 4, 32], F32, r_ab)
        b_in, at = place("b_in", [P, H], F32, at)

        wq_hi, at = place("wq_hi", [P, KC, H], F32R, r_w)
        wq_lo, at = place("wq_lo", [P, KC, H], F32R, at)
        at = r_w
        qst = [None, None]
        for par in range(2):
            qst[par], at = place(f"q_stack{par}", [P, NKV, QH], F32R, at)
        probs, at = place("probs", [TR, TC, JH, QH], F32, at)
        prob_sum, at = place("prob_sum", [TR, JH, QH], F32, at)
        inv_den, at = place("inv_den", [P, QH], F32, at)
        attn = [None, None]
        for h in range(HALVES):
            attn[h], at = place(f"attn{h}", [P, RH, NQ], F32, at)
        assert at <= r_kv

        wk_hi, at = place("wk_hi", [P, KC, KVW], F32R, r_kv)
        wk_lo, at = place("wk_lo", [P, KC, KVW], F32R, at)
        wv_hi, at = place("wv_hi", [P, KC, KVW], F32R, at)
        wv_lo, at = place("wv_lo", [P, KC, KVW], F32R, at)
        xt_hi, at = place("xt_hi", [P, KC, QG * NQ], F32R, r_ct)
        xt_lo, at = place("xt_lo", [P, KC, QG * NQ], F32R, at)
        ct_hi, at = place("ct_hi", [P, KC, NTE], F32R, r_ct)
        ct_lo, at = place("ct_lo", [P, KC, NTE], F32R, r_ct + KC * QG * NQ * 4)
        ctx_in, at = place("ctx_in", [TR, TC, H], F32, r_cin)
        wo_hi, at = place("wo_hi", [P, KC, H], F32R, r_kv)
        wo_lo, at = place("wo_lo", [P, KC, H], F32R, r_ct)
        assert at <= r_ks

        kst, v_sb = [None, None], [None, None]
        at = r_ks
        for par in range(2):
            kst[par], at = place(f"k_stack{par}", [P, NKV, NTE], F32R, at)
        at = r_v
        for par in range(2):
            v_sb[par], at = place(f"v{par}", [TR, TC, KVW], F32, at)
        x_in, at = place("x_in", [NQ, QG, H], F32, r_x)
        qev_hi, at = place("q_out_hi", [P, QG, RH, NQ], F32R, at)
        qev_lo, at = place("q_out_lo", [P, QG, RH, NQ], F32R, at)

        def staging(tag, at):
            raw = [None, None]
            wsum = [None, None]
            for par in range(2):
                raw[par], at = place(f"w_raw{tag}{par}", [P, WBLK], F32, at)
                wsum[par], at = place(f"w_sum{tag}{par}", [P, WBLK], F32, at)
            a_st, at = place(f"a_stack{tag}", [P, KC, P], F32R, at)
            b_st, at = place(f"b_stack{tag}", [P, H], F32R, at)
            return raw, wsum, a_st, b_st, at

        raw1, wsum1, ast1, bst1, at = staging("_qkv", r_ks)
        assert at <= r_x
        raw2, wsum2, ast2, bst2, at = staging("_o", r_x)
        assert at <= top[0]

        at_raw, at_hi, at_lo, res = [None, None], [None, None], [None, None], [None, None]
        for par in range(2):
            at = r_w + par * NKV * QH * 4
            at_raw[par], at = place(f"attn_rows{par}", [P, KC, P], F32, at)
            at_hi[par], at = place(f"attn_hi{par}", [P, KC, P], F32R, at)
            at_lo[par], at = place(f"attn_lo{par}", [P, KC, P], F32R, at)
            res[par], at = place(f"residual{par}", [P, H], F32, r_ks + par * NKV * NTE * 4)

        ps = stack.enter_context(nc.psum_tensor("ps", [P, 8, BANK], F32))

        q_scr = nc.dram_tensor("q_scratch", [2, B, HALVES, P, QH], F32, kind="Internal").ap()
        at_scr = nc.dram_tensor("attn_scratch", [P, KC, ROWS], F32, kind="Internal").ap()

        def sem(name):
            return stack.enter_context(nc.semaphore(name))

        zeroed = sem("zeroed")
        ident_set = sem("ident_set")
        ones_row = sem("ones_row")
        ab_in = sem("ab_in")
        raw_in = [sem("raw_in0"), sem("raw_in1")]
        a_placed_pad = sem("a_pads")
        a_placed = sem("a_placed")
        a_turned = sem("a_turned")
        a_hi = sem("a_hi")
        a_lo = sem("a_lo")
        b_hi = sem("b_hi")
        b_lo = sem("b_lo")
        folded = sem("folded")
        w_summed = sem("w_summed")
        w_hi = sem("w_hi")
        w_lo = [sem("w_lo_dve"), sem("w_lo_pool")]
        x_loaded = sem("x_loaded")
        xt_turned = sem("xt_turned")
        xt_hi_set = sem("xt_hi_set")
        xt_lo_set = sem("xt_lo_set")
        q_done = sem("q_done")
        q_hi_set = sem("q_hi_set")
        q_lo_set = sem("q_lo_set")
        q_stored = sem("q_stored")
        ctx_loaded = sem("ctx_loaded")
        ct_turned = sem("ct_turned")
        ct_hi_set = sem("ct_hi_set")
        ct_lo_set = sem("ct_lo_set")
        k_done = sem("k_done")
        k_hi_set = sem("k_hi_set")
        k_lo_set = sem("k_lo_set")
        v_done = sem("v_done")
        v_set = sem("v_set")
        q_in = [[sem(f"q_in{h}{par}") for par in range(2)] for h in range(HALVES)]
        nat_done = sem("nat_done")
        max_done = sem("max_done")
        m_turned = sem("m_turned")
        m_neg = sem("m_neg")
        m_in = [sem("m_in0"), sem("m_in1")]
        st_done = sem("st_done")
        exp_done = sem("exp_done")
        pv_done = sem("pv_done")
        psum_added = sem("prob_sums")
        den_done = sem("den_done")
        inv_set = sem("inv_set")
        attn_set = sem("attn_set")
        attn_stored = [sem("attn_stored0"), sem("attn_stored1")]
        at_in = [sem("at_in0"), sem("at_in1")]
        res_in = [sem("res_in0"), sem("res_in1")]
        at_hi_set = sem("at_hi_set")
        at_lo_set = sem("at_lo_set")
        o_done = sem("o_done")
        o_added = sem("o_added")
        out_stored = [sem("out_stored0"), sem("out_stored1")]

        block = stack.enter_context(nc.Block())

        x_rows = x.rearrange("b q n -> (b q) n")
        out_rows = out.rearrange("b q n -> (b q) n")

        def ct_bank(b, k):
            return NAT + k % 2 if isinstance(b, int) and b == 0 else TURN

        def q_bank(g, c):
            first = isinstance(g, int) and g == 0 and c in (2, 3)
            return CTX + c % 2 if first else DENSE + c % 2

        def natural(w):
            return w.rearrange("(k p) n -> k p n", p=P)

        W_ALL = [
            (Wq, Aq, Bq, H), (Wk, Ak, Bk, KVW), (Wv, Av, Bv, KVW), (Wo, Ao, Bo, H),
        ]
        W_O = 3
        FIRST_BLOCK = [0, KC, KC + 2, KC + 4, 2 * KC + 4]
        QKV_BLOCKS = FIRST_BLOCK[W_O]

        AB_LOADS = [16 * 5, 16 * 10, 16 * 15, 16 * (15 + KC * JH + 4)]
        RAW_LOADS = []
        for g in range(FIRST_BLOCK[4]):
            before = RAW_LOADS[g - 2] if g >= 2 else 0
            RAW_LOADS.append(before + 16 * (JH if g >= QKV_BLOCKS else 1))

        def lo_by_pool(g):
            return int(g % 2 == 1 and not KC <= g < QKV_BLOCKS)

        def lo_count(g):
            return sum(lo_by_pool(n) == lo_by_pool(g) for n in range(g + 1))

        def wait_lo(eng, g):
            eng.wait_ge(w_lo[lo_by_pool(g)], lo_count(g))

        def wait_qkv(eng):
            wait_lo(eng, QKV_BLOCKS - 1)
            wait_lo(eng, KC - 1)

        def w_block(w, n):
            if w == 0:
                return wq_hi[:, n, :], wq_lo[:, n, :]
            if w == W_O:
                return wo_hi[:, n, :], wo_lo[:, n, :]
            hi, lo = (wk_hi, wk_lo) if w == 1 else (wv_hi, wv_lo)
            return (t[:, 4 * n:4 * n + 4, :].rearrange("p k n -> p (k n)") for t in (hi, lo))

        def run_steps(eng, step, wo_factors):
            full = ({"A", "D", "V", "T", "N", "Q"}, {"A", "D", "T", "K", "C", "N", "Q"})
            step(-1, 0, (set(), {"K", "C"}))
            wo_factors()
            step(-1, 1, ({"V", "T", "N"}, {"T", "K", "C", "N"}))
            step(0, 0, (full[0] - {"D"}, full[1]))
            with eng.Fori(0, (B - 4) // 2) as pair:
                step(pair, 1, full)
                step(pair, 2, full)
            step(B // 2 - 2, 1, (full[0], full[1] - {"C"}))
            step(B // 2 - 1, 0, ({"A", "D", "V", "N"}, {"A", "D", "N", "W0"}))
            step(B // 2 - 1, 1, ({"A", "D", "W1"}, {"A", "D", "W2"}))

        @block.sync
        def _(sp):
            def load_ab(w):
                W, A, Bm, width = W_ALL[w]
                if w:
                    sp.wait_ge(a_placed, w)
                    sp.wait_ge(b_lo, w)
                if w == W_O:
                    for c in range(KC):
                        half, r = c // RH, c % RH
                        for j in range(JH):
                            row = ((half * JH + j) * RH + r) * HD
                            sp.dma_start(a_in[j * HD:(j + 1) * HD, c, :], A[row:row + HD, :]).then_inc(ab_in, 16)
                else:
                    sp.dma_start(a_in[:, :, :], A.rearrange("(k p) r -> p k r", p=P)).then_inc(ab_in, 16)
                for quad in range(4):
                    sp.dma_start(b_in[32 * quad:32 * quad + R, 0:width], Bm).then_inc(ab_in, 16)

            def load_raw(w, n):
                W = W_ALL[w][0]
                g = FIRST_BLOCK[w] + n
                raw = raw2 if w == W_O else raw1
                if g >= 2:
                    sp.wait_ge(w_summed, g - 1)
                if w == W_O:
                    half, r = n // RH, n % RH
                    for j in range(JH):
                        row = ((half * JH + j) * RH + r) * HD
                        sp.dma_start(raw[g % 2][j * HD:(j + 1) * HD, :], W[row:row + HD, :]).then_inc(raw_in[g % 2], 16)
                elif w == 0:
                    sp.dma_start(raw[g % 2][:, :], W[n * P:(n + 1) * P, :]).then_inc(raw_in[g % 2], 16)
                else:
                    sp.dma_start(raw[g % 2][:, :].rearrange("p (k n) -> p k n", k=4),
                                 W[n * 4 * P:(n + 1) * 4 * P, :].rearrange("(k p) n -> p k n", p=P)
                                 ).then_inc(raw_in[g % 2], 16)

            def load_x(g):
                sp.dma_start(x_in[:, :, :], x[bass.ds(g * QG, QG), :, :].rearrange("b q n -> q b n")
                             ).then_inc(x_loaded, 16)

            def load_ctx(b):
                sp.dma_start(ctx_in[:, :, :],
                             ctxt[bass.ds(b, 1), :, :].rearrange("b (t p) n -> p (b t) n", p=TR)
                             ).then_inc(ctx_loaded, 16)

            sp.wait_ge(zeroed, 1)
            load_ab(0)
            load_raw(0, 0)
            load_raw(0, 1)
            load_x(0)
            for n in range(2, KC):
                load_raw(0, n)
            load_ab(1)
            for n in range(2):
                load_raw(1, n)

            def store_q(g, half):
                sp.wait_ge(q_lo_set, g * 2 * RH + (half + 1) * RH)
                for hl, t in ((0, qev_hi), (1, qev_lo)):
                    sp.dma_start(q_scr[hl, bass.ds(g * QG, QG), half, :, :].rearrange("b p n -> p b n"),
                                 t[:, :, :, :].bitcast(F32).rearrange("p b r q -> p b (r q)")
                                 ).then_inc(q_stored, 16)

            def next_x(g):
                sp.wait_ge(xt_turned, (g + 1) * KC)
                load_x(g + 1)

            next_x(0)
            store_q(0, 0)
            load_ab(2)
            for n in range(2):
                load_raw(2, n)
            store_q(0, 1)
            load_ctx(0)
            with sp.Fori(1, GROUPS - 1) as g:
                next_x(g)
                store_q(g, 0)
                store_q(g, 1)
            store_q(GROUPS - 1, 0)
            store_q(GROUPS - 1, 1)

            def load_q(pair, off, h):
                b = 2 * pair + off
                for n, hl in enumerate((0, 1, 0)):
                    sp.dma_start(qst[off % 2][32 * n:32 * n + HD, h * JH:(h + 1) * JH, :].bitcast(F32),
                                 q_scr[hl, bass.ds(b, 1), h, :, :].rearrange("b (j d) n -> d (b j) n", d=HD)
                                 ).then_inc(q_in[h][off % 2], 16)

            sp.wait_ge(q_stored, GROUPS * HALVES * 32)
            sp.wait_ge(q_done, GROUPS * 2 * RH)
            for off in range(2):
                for h in range(HALVES):
                    load_q(0, off, h)

            def store_attn(b, h):
                sp.wait_ge(attn_set, 2 * b + h + 1)
                sp.dma_start(at_scr[:, h * RH:(h + 1) * RH, bass.ds(b * NQ, NQ)], attn[h][:, :, :]
                             ).then_inc(attn_stored[h], 16)

            def load_tile(pair, par, first=False):
                t = 2 * pair + par
                if first:
                    sp.wait_ge(st_done, 2 * NS * (B - 1 + par))
                    for h in range(HALVES):
                        sp.wait_ge(attn_stored[h], 16 * 3)
                else:
                    sp.wait_ge(at_lo_set, t - 1)
                sp.dma_start(at_raw[par][:, :, :], at_scr[:, :, bass.ds(t * P, P)]).then_inc(at_in[par], 16)
                if not first:
                    sp.wait_ge(out_stored[par], 16 * pair)
                sp.dma_start(res[par][:, :], x_rows[bass.ds(t * P, P), :]).then_inc(res_in[par], 16)

            def store_tile(pair, par):
                t = 2 * pair + par
                sp.wait_ge(o_added, 2 * t + 2)
                sp.dma_start(out_rows[bass.ds(t * P, P), :], res[par][:, :]).then_inc(out_stored[par], 16)

            def step(pair, off, has):
                b = 2 * pair + off
                for h in range(HALVES):
                    if "W1" in has[h]:
                        load_tile(0, 0, True)
                    for kind, i, k in half_order(h, has[h]):
                        if kind == "A":
                            if h == 0:
                                store_attn(b - 1, 1)
                            else:
                                store_attn(b, 0)
                        elif kind == "K" and i == 1 and k == 0 and "C" in has[h]:
                            sp.wait_ge(ct_turned, (b + 3) * KC)
                            load_ctx(b + 3)
                        elif kind == "M":
                            sp.wait_ge(m_neg, 2 * (b + 1) + h + 1)
                            sp.dma_start(qst[(off + 1) % 2][STK:STM, h * JH:(h + 1) * JH, :].bitcast(F32)
                                         .rearrange("p j (r q) -> p (j r) q", r=RH),
                                         neg_max[:, h, :].bitcast(F32)).then_inc(m_in[h], 16)
                        elif kind == "W" and i + 1 in range(2, KC):
                            load_raw(W_O, i + 1)
                        elif kind == "E" and "Q" in has[h]:
                            sp.wait_ge(st_done, NS * (2 * b + h + 1))
                            load_q(pair, off + 2, h)

            def wo_factors():
                load_ab(W_O)
                load_raw(W_O, 0)
                load_raw(W_O, 1)

            run_steps(sp, step, wo_factors)
            load_tile(0, 1, True)
            store_attn(B - 1, 1)
            for h in range(HALVES):
                sp.wait_ge(attn_stored[h], 16 * B)
            with sp.Fori(0, OT // 2 - 1) as pair:
                for par in range(2):
                    store_tile(pair, par)
                    load_tile(pair + 1, par)
            for par in range(2):
                store_tile(OT // 2 - 1, par)
            for par in range(2):
                sp.wait_ge(out_stored[par], 16 * (OT // 2))

        @block.gpsimd
        def _(pool):
            def pool_lo(w, n):
                g = FIRST_BLOCK[w] + n
                pool.wait_ge(w_hi, g + 1)
                hi, lo = w_block(w, n)
                pool.tensor_tensor(lo, (wsum2 if w == W_O else wsum1)[g % 2][:, :], hi, ALU.subtract
                                   ).then_inc(w_lo[1], 1)

            pool.memset(b_in[:, :], 0.0).then_inc(zeroed, 1)
            pool.memset(ident[:, :], 0.0).then_inc(ident_set, 1)
            pool.wait_ge(ident_set, 1)
            pool.affine_select(out=ident[:, :], in_=ident[:, :], compare_op=ALU.not_equal, fill=1.0, base=0,
                               pattern=[[-1, P]], channel_multiplier=1).then_inc(ident_set, 1)
            pool.memset(ones[:, :], 1.0).then_inc(ident_set, 1)
            for n in range(1, KC, 2):
                pool_lo(0, n)
            wait_qkv(pool)
            for par in range(2):
                pool.memset(kst[par][STK:STM, :, :].bitcast(F32), 1.0).then_inc(ones_row, 1)
                pool.wait_ge(ones_row, par + 1)
            pool.wait_ge(q_done, GROUPS * 2 * RH)
            for par, t in enumerate((ct_hi, ct_lo)):
                pool.memset(t[:, :, NT:NTE].bitcast(F32), 0.0).then_inc(ones_row, 1)
                pool.wait_ge(ones_row, par + 3)

            def step(pair, off, has):
                b = 2 * pair + off
                for h in range(HALVES):
                    n = 2 * b + h
                    for kind, i, k in half_order(h, has[h]):
                        if kind == "S" and i == 2 * JH - 1:
                            at_least(pool, den_done, n)
                            pool.wait_ge(exp_done, NS * n + 2 * JH)
                            pool.tensor_tensor(prob_sum[:, :, :], probs[:, 0, :, :], probs[:, 1, :, :], ALU.add
                                               ).then_inc(psum_added, 1)
                        elif kind == "S" and i == NS - 1:
                            pool.wait_ge(psum_added, 2 * n + 1)
                            pool.wait_ge(exp_done, NS * (n + 1))
                            pool.tensor_tensor(prob_sum[:, :, :], prob_sum[:, :, :], probs[:, 2, :, :], ALU.add
                                               ).then_inc(psum_added, 1)
                        elif kind == "W" and lo_by_pool(QKV_BLOCKS + i):
                            pool_lo(W_O, i)

            run_steps(pool, step, lambda: None)

        @block.tensor
        def _(pe):
            pe.wait_ge(ident_set, 3)

            def mm3(dst, l_hi, l_lo, r_hi, r_lo, start, stop):
                pe.matmul(dst, l_hi, r_hi, start=start, stop=False)
                pe.matmul(dst, l_hi, r_lo, start=False, stop=False)
                return pe.matmul(dst, l_lo, r_hi, start=False, stop=stop)

            def turn_a(w, bank):
                if w:
                    pe.wait_ge(w_summed, FIRST_BLOCK[w])
                pe.wait_ge(a_placed, w + 1)
                for k in range(KC):
                    mm = pe.transpose(ps[:, bank + k // 4, (k % 4) * P:(k % 4 + 1) * P],
                                      a_dup[:, k, :, :].rearrange("p a r -> p (a r)"), ident[:, :])
                mm.then_inc(a_turned, 1)

            def fold(w, n, bank):
                g = FIRST_BLOCK[w] + n
                width = W_ALL[w][3]
                a_st, b_st = (ast2, bst2) if w == W_O else (ast1, bst1)
                if n == 0:
                    pe.wait_ge(a_lo, w + 1)
                    pe.wait_ge(b_lo, w + 1)
                else:
                    pe.wait_ge(w_summed, g)
                for m in range(2):
                    if width == H:
                        mm = pe.matmul(ps[:, bank + m, :], a_st[:, n, :], b_st[:, m * BANK:(m + 1) * BANK],
                                       start=True, stop=True)
                    else:
                        for k in range(2):
                            mm = pe.matmul(ps[:, bank + m, k * KVW:(k + 1) * KVW], a_st[:, 4 * n + 2 * m + k, :],
                                           b_st[:, 0:KVW], start=True, stop=True)
                mm.then_inc(folded, 1)

            def turn_x(g, k):
                if k == 0:
                    pe.wait_ge(x_loaded, 16 * g + 16)
                at_least(pe, xt_lo_set, g * KC + k - 1)
                for b in range(QG):
                    mm = pe.transpose(ps[:, NAT + k % 2, b * NQ:(b + 1) * NQ], x_in[:, b, k * P:(k + 1) * P],
                                      ident[0:NQ, 0:NQ])
                mm.then_inc(xt_turned, 1)

            def q_piece(g, c, k):
                cols = slice(c * P, (c + 1) * P)
                return mm3(ps[:, q_bank(g, c), 0:QG * NQ], wq_hi[:, k, cols], wq_lo[:, k, cols],
                           xt_hi[:, k, :], xt_lo[:, k, :], k == 0, k == KC - 1)

            def q_chunk(g, c):
                if c >= 1:
                    pe.wait_ge(q_lo_set, g * 2 * RH + c - 1)
                for k in range(KC):
                    if c == 0:
                        pe.wait_ge(xt_lo_set, g * KC + k + 1)
                    mm = q_piece(g, c, k)
                    if c == 2 * RH - 1:
                        if k == KC - 1:
                            mm.then_inc(q_done, 1)
                        if isinstance(g, int) and g == GROUPS - 1:
                            turn_ctx(0, k)
                        else:
                            turn_x(g + 1, k)
                if c < 2 * RH - 1:
                    mm.then_inc(q_done, 1)

            def turn_ctx(b, k):
                if k == 0:
                    pe.wait_ge(ctx_loaded, 16 * (b + 1))
                bank = ct_bank(b, k)
                if bank != TURN:
                    at_least(pe, ct_lo_set, k - 1)
                elif k == 0:
                    pe.wait_ge(k_lo_set, 2 * b)
                else:
                    pe.wait_ge(ct_lo_set, b * KC + k)
                for t in range(TC):
                    mm = pe.transpose(ps[:, bank, t * TR:(t + 1) * TR], ctx_in[:, t, k * P:(k + 1) * P],
                                      ident[0:TR, 0:TR])
                mm.then_inc(ct_turned, 1)

            def q_first(k):
                wait_lo(pe, k)
                pe.wait_ge(xt_lo_set, k + 1)
                for c in range(4):
                    mm = q_piece(0, c, k)
                    if k == KC - 1:
                        mm.then_inc(q_done, 1)

            turn_a(0, FOLD)
            for k in range(KC):
                turn_x(0, k)
                fold(0, k, FOLD)
                if k:
                    q_first(k - 1)
            q_first(KC - 1)
            turn_a(1, FOLD)
            q_chunk(0, 4)
            fold(1, 0, FOLD)
            q_chunk(0, 5)
            fold(1, 1, FOLD)
            turn_a(2, FOLD)
            q_chunk(0, 6)
            fold(2, 0, FOLD)
            q_chunk(0, 7)
            fold(2, 1, FOLD)
            pe.wait_ge(q_lo_set, 2 * RH - 1)
            with pe.Fori(1, GROUPS - 1) as g:
                for c in range(2 * RH):
                    q_chunk(g, c)
                pe.wait_ge(q_lo_set, g * 2 * RH + 2 * RH - 1)
            for c in range(2 * RH):
                q_chunk(GROUPS - 1, c)
            pe.wait_ge(q_lo_set, GROUPS * 2 * RH)
            wait_qkv(pe)
            pe.wait_ge(ones_row, 4)

            def step(pair, off, has):
                b = 2 * pair + off
                cur, nxt = off % 2, (off + 1) % 2
                for h in range(HALVES):
                    n = 2 * b + h
                    m = 2 * (b + 1) + h
                    for kind, i, k in half_order(h, has[h]):
                        if kind == "V":
                            if k == 0 and i == 0:
                                at_least(pe, k_lo_set, 2 * (b + 1) + 1)
                            dst = ps[0:TR, VA + i // 2, (i % 2) * KVW:(i % 2 + 1) * KVW]
                            rows = slice(i * TR, (i + 1) * TR)
                            pe.matmul(dst, ct_hi[:, k, rows], wv_hi[:, k, :], start=(k == 0 and i != 1), stop=False,
                                      skip_group_check=True)
                            pe.matmul(dst, ct_hi[:, k, rows], wv_lo[:, k, :], start=False, stop=False,
                                      skip_group_check=True)
                            mm = pe.matmul(dst, ct_lo[:, k, rows], wv_hi[:, k, :], start=False,
                                           stop=(k == KC - 1), skip_group_check=True)
                            if k == KC - 1 and i >= 1:
                                mm.then_inc(v_done, 1)
                        elif kind == "T":
                            turn_ctx(b + 2, i)
                        elif kind == "K":
                            if k == 0:
                                at_least(pe, v_set, 2 * (b + 1) + 2)
                                if i == 1:
                                    pe.wait_ge(ct_lo_set, (b + 3) * KC)
                            if i == 0:
                                pe.wait_ge(ct_lo_set, (b + 2) * KC + k + 1)
                            cols = slice(i * P, (i + 1) * P)
                            mm = mm3(ps[:, (VA, TURN)[i], 0:NTE], wk_hi[:, k, cols], wk_lo[:, k, cols],
                                     ct_hi[:, k, :], ct_lo[:, k, :], k == 0, k == KC - 1)
                            if k == KC - 1:
                                mm.then_inc(k_done, 1)
                        elif kind == "S":
                            if i == 0:
                                pe.wait_ge(m_in[h], 16 * (b + 1))
                            at_least(pe, exp_done, NS * n + i)
                            g, c = h * JH + i % JH, i // JH
                            pe.matmul(ps[0:TR, STB, 0:QH], kst[cur][0:STM, g, c * TR:(c + 1) * TR],
                                      qst[cur][0:STM, g, :], start=True, stop=True).then_inc(st_done, 1)
                        elif kind == "N":
                            if i == 0:
                                pe.wait_ge(q_in[h][nxt], 48 * (pair + (off + 1) // 2 + 1))
                                pe.wait_ge(k_lo_set, m + 1)
                                at_least(pe, m_neg, m)
                            at_least(pe, max_done, 8 * m + i)
                            g, r0 = h * JH + i // 2, 2 * (i % 2)
                            for rr in range(2):
                                mm = pe.matmul(ps[0:NQ, NAT + rr, 0:NTE],
                                               qst[nxt][0:STK, g, (r0 + rr) * NQ:(r0 + rr + 1) * NQ],
                                               kst[nxt][0:STK, g, :], start=True, stop=True)
                            mm.then_inc(nat_done, 1)
                        elif kind == "M":
                            pe.wait_ge(max_done, 8 * m + 8)
                            pe.transpose(ps[0:JH * RH, NAT, 0:NQ], maxima[:, h, :], ident[0:NQ, 0:NQ]
                                         ).then_inc(m_turned, 1)
                        elif kind == "P":
                            pe.wait_ge(exp_done, NS * n + JH * (i + 1))
                            if i == 0:
                                at_least(pe, attn_set, n)
                                pe.wait_ge(v_set, 2 * (b + 1))
                            for j in range(JH):
                                g = h * JH + j
                                mm = pe.matmul(ps[HD * j:HD * (j + 1), CTX, 0:QH],
                                               v_sb[cur][:, i, g * HD:(g + 1) * HD], probs[:, i, j, :],
                                               start=(i == 0), stop=(i == TC - 1))
                            mm.then_inc(pv_done, 1)
                        elif kind == "D":
                            denominators(n - 1)
                        elif kind == "W":
                            if i == 0:
                                pe.wait_ge(v_set, 2 * B)
                            fold(W_O, i, FOLD_O)
                        elif kind == "O":
                            if i == 0:
                                pe.wait_ge(at_lo_set, 1)
                                pe.wait_ge(m_neg, 2 * B)
                            wait_lo(pe, QKV_BLOCKS + i)
                            for m in range(2):
                                o_piece(0, m, i, NAT).then_inc(o_done, 1) if i == KC - 1 else o_piece(0, m, i, NAT)

            def o_piece(par, m, k, bank):
                cols = slice(m * BANK, (m + 1) * BANK)
                return mm3(ps[:, bank + m, :], at_hi[par][:, k, :], at_lo[par][:, k, :],
                           wo_hi[:, k, cols], wo_lo[:, k, cols], k == 0, k == KC - 1)

            def denominators(n):
                pe.wait_ge(psum_added, 2 * n + 2)
                at_least(pe, inv_set, RH * n)
                for j in range(JH):
                    mm = pe.matmul(ps[HD * j:HD * (j + 1), DEN, 0:QH], ones[:, :], prob_sum[:, j, :],
                                   start=True, stop=True)
                mm.then_inc(den_done, 1)

            def wo_factors():
                turn_a(W_O, FOLD)

            run_steps(pe, step, wo_factors)
            denominators(2 * B - 1)

            def tile(pair, par):
                t = 2 * pair + par
                pe.wait_ge(at_lo_set, t + 1)
                for m in range(2):
                    at_least(pe, o_added, 2 * t + m - 1)
                    for k in range(KC):
                        mm = o_piece(par, m, k, DENSE)
                    mm.then_inc(o_done, 1)

            wait_lo(pe, FIRST_BLOCK[4] - 1)
            tile(0, 1)
            with pe.Fori(1, OT // 2) as pair:
                tile(pair, 0)
                tile(pair, 1)

        @block.scalar
        def _(act):
            def ab_hi(w, bank):
                a_st, b_st = (ast2, bst2) if w == W_O else (ast1, bst1)
                width = W_ALL[w][3]
                act.wait_ge(ab_in, AB_LOADS[w])
                at_least(act, folded, FIRST_BLOCK[w])
                act.activation(b_st[:, 0:width], b_in[:, 0:width], ACT.Copy).then_inc(b_hi, 1)
                act.wait_ge(a_turned, w + 1)
                act.activation(a_st[:, :, :].rearrange("p k n -> p (k n)"),
                               ps[:, bank:bank + 2, :].rearrange("p a n -> p (a n)"), ACT.Copy, scale=LORA
                               ).then_inc(a_hi, 1)

            def block_hi(w, n):
                g = FIRST_BLOCK[w] + n
                act.wait_ge(w_summed, g + 1)
                hi, lo = w_block(w, n)
                act.activation(hi, (wsum2 if w == W_O else wsum1)[g % 2][:, :], ACT.Copy).then_inc(w_hi, 1)

            def x_hi(g, k):
                act.wait_ge(xt_turned, g * KC + k + 1)
                act.activation(xt_hi[:, k, :], ps[:, NAT + k % 2, 0:QG * NQ], ACT.Copy).then_inc(xt_hi_set, 1)

            def q_hi(g, c):
                if c % RH == 0:
                    at_least(act, q_stored, 32 * (2 * g + c // RH))
                act.wait_ge(q_done, g * 2 * RH + c + 1)
                act.activation(qev_hi[:, :, c % RH, :],
                               ps[:, q_bank(g, c), 0:QG * NQ].rearrange("p (b q) -> p b q", b=QG), ACT.Copy
                               ).then_inc(q_hi_set, 1)

            def ctx_hi(b, k):
                act.wait_ge(ct_turned, b * KC + k + 1)
                act.activation(ct_hi[:, k, 0:NT], ps[:, ct_bank(b, k), 0:NT], ACT.Copy).then_inc(ct_hi_set, 1)

            ab_hi(0, FOLD)
            for k in range(KC):
                x_hi(0, k)
                block_hi(0, k)
            ab_hi(1, FOLD)
            for c in range(4):
                q_hi(0, c)
            q_hi(0, 4)
            block_hi(1, 0)
            q_hi(0, 5)
            block_hi(1, 1)
            ab_hi(2, FOLD)
            q_hi(0, 6)
            block_hi(2, 0)
            for k in range(KC):
                x_hi(1, k)
            q_hi(0, 7)
            block_hi(2, 1)
            with act.Fori(1, GROUPS - 1) as g:
                for c in range(2 * RH - 1):
                    q_hi(g, c)
                for k in range(KC):
                    x_hi(g + 1, k)
                q_hi(g, 2 * RH - 1)
            for c in range(2 * RH - 1):
                q_hi(GROUPS - 1, c)
            for k in range(KC):
                ctx_hi(0, k)
            q_hi(GROUPS - 1, 2 * RH - 1)

            def step(pair, off, has):
                b = 2 * pair + off
                cur, nxt = off % 2, (off + 1) % 2
                for h in range(HALVES):
                    n = 2 * b + h
                    m = 2 * (b + 1) + h
                    for kind, i, k in half_order(h, has[h]):
                        if kind == "V" and k == KC - 1 and i >= 1:
                            act.wait_ge(v_done, 2 * (b + 1) + i)
                            wide = 2 * KVW if i == 1 else KVW
                            c0 = 0 if i == 1 else 2
                            act.activation(v_sb[nxt][:, c0:i + 1, :].rearrange("p c n -> p (c n)"),
                                           ps[0:TR, VA + i // 2, 0:wide], ACT.Copy).then_inc(v_set, 1)
                        elif kind == "T":
                            ctx_hi(b + 2, i)
                        elif kind == "K" and k == KC - 1:
                            act.wait_ge(k_done, 2 * (b + 2) + i + 1)
                            at_least(act, st_done, NS * (2 * b + i + 1))
                            for j in range(JH):
                                for quad in range(2):
                                    op = act.activation(kst[cur][HD * quad:HD * (quad + 1), i * JH + j, :],
                                                        ps[HD * j:HD * (j + 1), (VA, TURN)[i], 0:NTE], ACT.Copy)
                            op.then_inc(k_hi_set, 1)
                        elif kind == "S":
                            c, j = i // JH, i % JH
                            act.wait_ge(st_done, NS * n + i + 1)
                            at_least(act, pv_done, 3 * n + c - 2)
                            at_least(act, psum_added, 2 * n - (1 if c < 2 else 0))
                            act.activation(probs[:, c, j, :], ps[0:TR, STB, 0:QH], ACT.Exp, scale=SM
                                           ).then_inc(exp_done, 1)
                        elif kind == "M":
                            act.wait_ge(m_turned, m + 1)
                            at_least(act, m_in[h], 16 * (b + 1))
                            act.activation(neg_max[:, h, :], ps[0:JH * RH, NAT, 0:NQ], ACT.Copy, scale=-1.0
                                           ).then_inc(m_neg, 1)
                        elif kind == "W":
                            block_hi(W_O, i)
                        elif kind == "O" and i == 0:
                            split(0, 0)

            def split(pair, par):
                t = 2 * pair + par
                act.wait_ge(at_in[par], 16 * (pair + 1))
                at_least(act, o_done, 2 * (t - 1))
                act.activation(at_hi[par][:, :, :], at_raw[par][:, :, :], ACT.Copy).then_inc(at_hi_set, 1)

            def wo_factors():
                act.wait_ge(q_stored, GROUPS * HALVES * 32)
                ab_hi(W_O, FOLD)

            run_steps(act, step, wo_factors)
            split(0, 1)
            with act.Fori(1, OT // 2) as pair:
                split(pair, 0)
                split(pair, 1)

        @block.vector
        def _(dve):
            dve.memset(a_dup[:, :, :, :].rearrange("p k a r -> p (k a r)"), 0.0).then_inc(a_placed_pad, 1)
            dve.wait_ge(a_placed_pad, 1)

            def ab_place(w):
                dve.wait_ge(ab_in, AB_LOADS[w])
                at_least(dve, a_turned, w)
                for quad in range(4):
                    op = dve.tensor_copy(a_dup[:, :, quad, 0:R], a_in[:, :, :])
                op.then_inc(a_placed, 1)

            def ab_lo(w, bank):
                a_st, b_st = (ast2, bst2) if w == W_O else (ast1, bst1)
                width = W_ALL[w][3]
                dve.wait_ge(b_hi, w + 1)
                dve.tensor_tensor(b_st[64:128, 0:width], b_in[64:128, 0:width], b_st[64:128, 0:width], ALU.subtract
                                  ).then_inc(b_lo, 1)
                dve.wait_ge(a_hi, w + 1)
                for quad in (1, 3):
                    rows = slice(32 * quad, 32 * quad + 32)
                    st = a_st[rows, :, :].rearrange("p k n -> p (k n)")
                    op = dve.scalar_tensor_tensor(out=st, in0=ps[rows, bank:bank + 2, :].rearrange("p a n -> p (a n)"),
                                                  scalar=LORA, in1=st, op0=ALU.mult, op1=ALU.subtract)
                op.then_inc(a_lo, 1)

            def block_sum(w, n, bank):
                g = FIRST_BLOCK[w] + n
                raw, wsum = (raw2, wsum2) if w == W_O else (raw1, wsum1)
                dve.wait_ge(folded, g + 1)
                dve.wait_ge(raw_in[g % 2], RAW_LOADS[g])
                if g >= 2:
                    wait_lo(dve, g - 2)
                if w == 0:
                    for m in range(2):
                        cols = slice(m * BANK, (m + 1) * BANK)
                        op = dve.tensor_tensor(
                            wsum[g % 2][:, cols].rearrange("p (r j d) -> p j r d", r=RH, j=JH),
                            ps[:, bank + m, :].rearrange("p (j r d) -> p j r d", j=JH, r=RH),
                            raw[g % 2][:, cols].rearrange("p (j r d) -> p j r d", j=JH, r=RH), ALU.add)
                else:
                    op = dve.tensor_tensor(wsum[g % 2][:, :], ps[:, bank:bank + 2, :].rearrange("p a n -> p (a n)"),
                                           raw[g % 2][:, :], ALU.add)
                op.then_inc(w_summed, 1)

            def block_lo(w, n):
                g = FIRST_BLOCK[w] + n
                if lo_by_pool(g):
                    return
                dve.wait_ge(w_hi, g + 1)
                hi, lo = w_block(w, n)
                dve.tensor_tensor(lo, (wsum2 if w == W_O else wsum1)[g % 2][:, :], hi, ALU.subtract
                                  ).then_inc(w_lo[0], 1)

            def x_lo(g, k):
                dve.wait_ge(xt_hi_set, g * KC + k + 1)
                dve.tensor_tensor(xt_lo[:, k, :], ps[:, NAT + k % 2, 0:QG * NQ], xt_hi[:, k, :], ALU.subtract
                                  ).then_inc(xt_lo_set, 1)

            def q_lo(g, c):
                dve.wait_ge(q_hi_set, g * 2 * RH + c + 1)
                dve.tensor_tensor(qev_lo[:, :, c % RH, :],
                                  ps[:, q_bank(g, c), 0:QG * NQ].rearrange("p (b q) -> p b q", b=QG),
                                  qev_hi[:, :, c % RH, :], ALU.subtract).then_inc(q_lo_set, 1)

            def ctx_lo(b, k):
                dve.wait_ge(ct_hi_set, b * KC + k + 1)
                dve.tensor_tensor(ct_lo[:, k, 0:NT], ps[:, ct_bank(b, k), 0:NT], ct_hi[:, k, 0:NT], ALU.subtract
                                  ).then_inc(ct_lo_set, 1)

            ab_place(0)
            ab_lo(0, FOLD)
            for k in range(KC):
                x_lo(0, k)
                block_sum(0, k, FOLD)
                if k:
                    block_lo(0, k - 1)
            block_lo(0, KC - 1)
            ab_place(1)
            ab_lo(1, FOLD)
            for c in range(5):
                q_lo(0, c)
            block_sum(1, 0, FOLD)
            block_lo(1, 0)
            q_lo(0, 5)
            block_sum(1, 1, FOLD)
            block_lo(1, 1)
            ab_place(2)
            ab_lo(2, FOLD)
            q_lo(0, 6)
            block_sum(2, 0, FOLD)
            block_lo(2, 0)
            for k in range(KC):
                x_lo(1, k)
            q_lo(0, 7)
            block_sum(2, 1, FOLD)
            block_lo(2, 1)
            with dve.Fori(1, GROUPS - 1) as g:
                for c in range(2 * RH - 1):
                    q_lo(g, c)
                for k in range(KC):
                    x_lo(g + 1, k)
                q_lo(g, 2 * RH - 1)
            for c in range(2 * RH - 1):
                q_lo(GROUPS - 1, c)
            for k in range(KC):
                ctx_lo(0, k)
            q_lo(GROUPS - 1, 2 * RH - 1)

            def invert(n, r):
                if r == 0:
                    dve.wait_ge(den_done, n + 1)
                cols = slice(r * NQ, (r + 1) * NQ)
                dve.reciprocal(inv_den[:, cols], ps[:, DEN, cols]).then_inc(inv_set, 1)

            def normalise(b, n, h):
                dve.wait_ge(inv_set, RH * (n + 1))
                dve.wait_ge(pv_done, 3 * (n + 1))
                at_least(dve, attn_stored[h], 16 * b)
                dve.tensor_tensor(attn[h][:, :, :].rearrange("p r q -> p (r q)"), ps[:, CTX, 0:QH], inv_den[:, :],
                                  ALU.mult).then_inc(attn_set, 1)

            def step(pair, off, has):
                b = 2 * pair + off
                cur = off % 2
                for h in range(HALVES):
                    n = 2 * b + h
                    m = 2 * (b + 1) + h
                    for kind, i, k in half_order(h, has[h]):
                        if kind == "T":
                            ctx_lo(b + 2, i)
                        elif kind == "K" and k == KC - 1:
                            dve.wait_ge(k_hi_set, 2 * (b + 2) + i + 1)
                            for j in range(JH):
                                op = dve.tensor_tensor(kst[cur][2 * HD:3 * HD, i * JH + j, :],
                                                       ps[HD * j:HD * (j + 1), (VA, TURN)[i], 0:NTE],
                                                       kst[cur][0:HD, i * JH + j, :], ALU.subtract)
                            op.then_inc(k_lo_set, 1)
                        elif kind == "N":
                            dve.wait_ge(nat_done, 8 * m + i + 1)
                            dve.tensor_reduce(maxima[:, h, 2 * i:2 * i + 2], ps[0:NQ, NAT:NAT + 2, 0:NT], AX.X,
                                              ALU.max).then_inc(max_done, 1)
                        elif kind == "R":
                            invert(n - 1, i)
                        elif kind == "A":
                            if h == 0:
                                normalise(b - 1, n - 1, 1)
                            else:
                                normalise(b, n - 1, 0)
                        elif kind == "W":
                            block_sum(W_O, i, FOLD_O)
                            block_lo(W_O, i)
                        elif kind == "O" and i == 0:
                            split(0, 0)

            def split(pair, par):
                dve.wait_ge(at_hi_set, 2 * pair + par + 1)
                dve.tensor_tensor(at_lo[par][:, :, :], at_raw[par][:, :, :], at_hi[par][:, :, :], ALU.subtract
                                  ).then_inc(at_lo_set, 1)

            def add_residual(pair, par):
                t = 2 * pair + par
                dve.wait_ge(res_in[par], 16 * (pair + 1))
                for m in range(2):
                    dve.wait_ge(o_done, 2 * t + m + 1)
                    part = res[par][:, m * BANK:(m + 1) * BANK]
                    bank = NAT if isinstance(pair, int) and t == 0 else DENSE
                    dve.tensor_tensor(part, ps[:, bank + m, :], part, ALU.add).then_inc(o_added, 1)

            def wo_factors():
                ab_place(W_O)
                ab_lo(W_O, FOLD)

            run_steps(dve, step, wo_factors)
            for r in range(RH):
                invert(2 * B - 1, r)
            normalise(B - 1, 2 * B - 1, 1)
            split(0, 1)
            add_residual(0, 0)
            split(1, 0)
            add_residual(0, 1)
            split(1, 1)
            with dve.Fori(1, OT // 2 - 1) as pair:
                for par in range(2):
                    add_residual(pair, par)
                    split(pair + 1, par)
            for par in range(2):
                add_residual(OT // 2 - 1, par)


_INS = ['x', 'ctx_4096', 'L0_xattn_Wq', 'L0_xattn_Aq', 'L0_xattn_Bq', 'L0_xattn_Wk', 'L0_xattn_Ak', 'L0_xattn_Bk',
        'L0_xattn_Wv', 'L0_xattn_Av', 'L0_xattn_Bv', 'L0_xattn_Wo', 'L0_xattn_Ao', 'L0_xattn_Bo']
_OUTS = [((B, NQ, H), 'float32')]


def kernel(**inputs):
    import numpy as _np
    import concourse.bacc as _bacc
    from concourse import mybir as _mybir
    from concourse.bass_utils import run_bass_kernel_spmd as _run

    nc = _bacc.Bacc("TRN2", target_bir_lowering=False, num_devices=1)
    arrays, args = {}, []
    for name in _INS:
        a = _np.ascontiguousarray(inputs[name])
        arrays[f"in_{name}_dram"] = a
        args.append(nc.dram_tensor(f"in_{name}_dram", a.shape, _mybir.dt.from_np(a.dtype), kind="ExternalInput").ap())
    for i, (shape, dtype) in enumerate(_OUTS):
        dt = _mybir.dt.from_np(_np.dtype(dtype))
        args.append(nc.dram_tensor(f"out_{i}_dram", shape, dt, kind="ExternalOutput").ap())
    xattn_kernel(nc, *args)
    r = _run(nc, [arrays], core_ids=[0])
    return r.results[0]["out_0_dram"]
```

```python
from contextlib import ExitStack

import concourse.bass as bass
from concourse import mybir

ALU = mybir.AluOpType
ACT = mybir.ActivationFunctionType
AX = mybir.AxisListType
F32 = mybir.dt.float32
F32R = mybir.dt.float32r

B, NQ, H = 16, 112, 1024
NT = 375
NH, NKV, HD = 32, 8, 32
R = 16
LORA = 32.0 / 16.0
P = 128
KC = H // P
HALVES = 2
JH = NKV // HALVES
RH = NH // NKV
QH = RH * NQ
KVW = NKV * HD
TC = 3
TR = NT // TC
NTE = NT + 1
QG = 4
GROUPS = B // QG
SM = 1.0 / float(HD) ** 0.5
ROWS = B * NQ
OT = ROWS // P
BANK = 512
WBLK = H
assert TR * TC == NT and QH <= BANK and OT * P == ROWS and GROUPS * QG == B

STK = 3 * HD
NS = TC * JH
NN = JH * RH
STM = STK + 1

NAT = 0
STB = 2
TURN = 3
VA, VB = 4, 5
CTX = 6
DEN = 7
S_IN_DEN = (3, 5, 7, 9, 11)
FOLD = 2
FOLD_O = 4
DENSE = 4

PLAN = sorted(
    [("S", i, 0.01 + 0.07 * i) for i in range(TC * JH)]
    + [("P", 0, 0.31), ("P", 1, 0.59), ("P", 2, 0.94), ("A", 0, 0.04), ("D", 0, 0.05)]
    + [("I", 0, 0.35), ("J", 0, 0.45)]
    + [("N", i, 0.03 + 0.052 * i) for i in range(JH * RH)] + [("M", 0, 0.90)]
    + [("E0", j, 0.62 + 0.08 * j) for j in range(JH)] + [("E1", j, 0.03 + 0.06 * j) for j in range(JH)],
    key=lambda item: item[2])
COST = {"S": QH, "P": 4 * QH, "D": 4 * QH, "N": NTE, "M": 2 * NQ, "V": 3 * KVW, "T": 2 * NT, "K": 3 * NTE,
        "W": 2 * BANK, "O": 6 * BANK}
LAG = 2
OLAG = 4


def half_order(h, has):
    dense = []
    if h == 0:
        for k in range(KC):
            dense += [("V", t, k) for t in range(TC) if "V" in has]
            dense += [("T", k - LAG, 0)] if "T" in has and k >= LAG else []
    if h == 1:
        for k in range(KC):
            dense += [("K", 0, k)] if "K" in has else []
            dense += [("T", KC - LAG + k // 2, 0)] if "T" in has and k % 2 == 0 and k // 2 < LAG else []
        dense += [("K", 1, k) for k in range(KC) if "K" in has]
    for name, first in (("W0", 0), ("W1", 4), ("W2", 8)):
        if name in has:
            for n in range(first, first + 4):
                dense += [("W", n, 0)] if n < KC else []
                dense += [("O", n - OLAG, 0)] if OLAG <= n < KC + OLAG else []
    need = {"S": "A", "P": "A", "D": "D", "A": "D", "I": "G", "J": "G", "N": "N", "M": "N", "E0": "K", "E1": "E1"}
    plan = [item for item in PLAN if need[item[0]] in has]
    order, at = [], 0
    total = sum(COST.get(piece[0], 0) for piece in dense + plan)
    for piece in dense:
        while plan and plan[0][2] * total <= at:
            order.append((plan[0][0], plan[0][1], 0))
            at += COST.get(plan.pop(0)[0], 0)
        order.append(piece)
        at += COST[piece[0]]
    order += [(kind, i, 0) for kind, i, _ in plan]
    assert "K" not in has or order.index(("K", 0, KC - 1)) < order.index(("E0", 0, 0))
    return order + [("E", 0, 0)]


def score_bank(i):
    return DEN if i in S_IN_DEN else STB


def at_least(eng, sem, n):
    if not isinstance(n, int) or n > 0:
        eng.wait_ge(sem, n)


def xattn_kernel(nc, x, ctxt, Wq, Aq, Bq, Wk, Ak, Bk, Wv, Av, Bv, Wo, Ao, Bo, out):
    stack = ExitStack()
    with stack:
        base = (nc.sbuf_base + 31) // 32 * 32
        limit = nc.sbuf_usable_end
        top = [base]

        def region(size):
            at = top[0]
            top[0] += (size + 31) // 32 * 32
            assert top[0] <= limit, (top[0], limit)
            return at

        def place(name, shape, dt, at):
            n = 4
            for s in shape[1:]:
                n *= s
            return nc.alloc_sbuf_tensor_at(name, shape, dt, offset=at), at + (n + 31) // 32 * 32

        r_small = region(512 + 128 + 128 + 2 * NQ * 4 + 512)
        r_ab = region(2 * 4 * H)
        r_w = region(2 * KC * H * 4)
        r_kv = region(4 * KC * KVW * 4)
        r_ct = region(2 * KC * QG * NQ * 4)
        r_cin = region(TC * H * 4)
        r_ks = region(2 * NKV * NTE * 4)
        r_v = region(2 * TC * KVW * 4)
        r_x = region(QG * H * 4 + 2 * QG * QH * 4)

        at = r_small
        ident, at = place("ident", [P, P], F32, at)
        ones, at = place("ones", [TR, HD], F32, at)
        maxima, at = place("maxima", [NQ, HALVES, JH * RH], F32, at)
        neg_max, at = place("neg_max", [JH * RH, HALVES, NQ], F32R, at)
        a_in, at = place("a_in", [P, KC, R], F32, at)
        a_dup, at = place("a_dup", [P, KC, 4, 32], F32, r_ab)
        b_in, at = place("b_in", [P, H], F32, at)

        wq_hi, at = place("wq_hi", [P, KC, H], F32R, r_w)
        wq_lo, at = place("wq_lo", [P, KC, H], F32R, at)
        at = r_w
        qst = [None, None]
        for par in range(2):
            qst[par], at = place(f"q_stack{par}", [P, NKV, QH], F32R, at)
        probs, at = place("probs", [TR, TC, JH, QH], F32, at)
        prob_sum, at = place("prob_sum", [TR, JH, QH], F32, at)
        den_sb, at = place("denominators", [P, QH], F32, at)
        den_rows, at = place("den_rows", [NH, NQ], F32, at)
        inv_rows, at = place("inv_rows", [NH, NQ], F32, at)
        attn = [None, None]
        for h in range(HALVES):
            attn[h], at = place(f"attn{h}", [P, RH, NQ], F32, at)
        assert at <= r_kv

        wk_hi, at = place("wk_hi", [P, KC, KVW], F32R, r_kv)
        wk_lo, at = place("wk_lo", [P, KC, KVW], F32R, at)
        wv_hi, at = place("wv_hi", [P, KC, KVW], F32R, at)
        wv_lo, at = place("wv_lo", [P, KC, KVW], F32R, at)
        xt_hi, at = place("xt_hi", [P, KC, QG * NQ], F32R, r_ct)
        xt_lo, at = place("xt_lo", [P, KC, QG * NQ], F32R, at)
        ct_hi, at = place("ct_hi", [P, KC, NTE], F32R, r_ct)
        ct_lo, at = place("ct_lo", [P, KC, NTE], F32R, r_ct + KC * QG * NQ * 4)
        ctx_in, at = place("ctx_in", [TR, TC, H], F32, r_cin)
        wo_hi, at = place("wo_hi", [P, KC, H], F32R, r_kv)
        wo_lo, at = place("wo_lo", [P, KC, H], F32R, r_ct)
        assert at <= r_ks

        kst, v_sb = [None, None], [None, None]
        at = r_ks
        for par in range(2):
            kst[par], at = place(f"k_stack{par}", [P, NKV, NTE], F32R, at)
        at = r_v
        for par in range(2):
            v_sb[par], at = place(f"v{par}", [TR, TC, KVW], F32, at)
        x_in, at = place("x_in", [NQ, QG, H], F32, r_x)
        qev_hi, at = place("q_out_hi", [P, QG, RH, NQ], F32R, at)
        qev_lo, at = place("q_out_lo", [P, QG, RH, NQ], F32R, at)

        def staging(tag, at):
            raw = [None, None]
            wsum = [None, None]
            for par in range(2):
                raw[par], at = place(f"w_raw{tag}{par}", [P, WBLK], F32, at)
                wsum[par], at = place(f"w_sum{tag}{par}", [P, WBLK], F32, at)
            a_st, at = place(f"a_stack{tag}", [P, KC, P], F32R, at)
            b_st, at = place(f"b_stack{tag}", [P, H], F32R, at)
            return raw, wsum, a_st, b_st, at

        raw1, wsum1, ast1, bst1, at = staging("_qkv", r_ks)
        assert at <= r_x
        raw2, wsum2, ast2, bst2, at = staging("_o", r_x)
        assert at <= top[0]

        at_raw, at_hi, at_lo, inv, res = ([None, None] for _ in range(5))
        for par in range(2):
            at = r_w + par * NKV * QH * 4
            at_raw[par], at = place(f"attn_rows{par}", [P, KC, P], F32, at)
            at_hi[par], at = place(f"attn_hi{par}", [P, KC, P], F32R, at)
            at_lo[par], at = place(f"attn_lo{par}", [P, KC, P], F32R, at)
            res[par], at = place(f"residual{par}", [P, H], F32, r_ks + par * NKV * NTE * 4)
            inv[par], at = place(f"inv_tile{par}", [P, KC, P], F32, at)

        ps = stack.enter_context(nc.psum_tensor("ps", [P, 8, BANK], F32))

        q_scr = nc.dram_tensor("q_scratch", [2, B, HALVES, P, QH], F32, kind="Internal").ap()
        at_scr = nc.dram_tensor("attn_scratch", [P, KC, ROWS], F32, kind="Internal").ap()

        den_scr = nc.dram_tensor("den_scratch", [NH, ROWS], F32, kind="Internal").ap()
        inv_scr = nc.dram_tensor("inv_scratch", [NH, ROWS], F32, kind="Internal").ap()

        def sem(name):
            return stack.enter_context(nc.semaphore(name))

        zeroed = sem("zeroed")
        ident_set = sem("ident_set")
        ones_row = sem("ones_row")
        ab_in = sem("ab_in")
        raw_in = [sem("raw_in0"), sem("raw_in1")]
        a_placed_pad = sem("a_pads")
        a_placed = sem("a_placed")
        a_turned = sem("a_turned")
        a_hi = sem("a_hi")
        a_lo = sem("a_lo")
        b_hi = sem("b_hi")
        b_lo = sem("b_lo")
        folded = sem("folded")
        w_summed = sem("w_summed")
        w_hi = sem("w_hi")
        w_lo = [sem("w_lo_dve"), sem("w_lo_pool")]
        x_loaded = sem("x_loaded")
        xt_turned = sem("xt_turned")
        xt_hi_set = sem("xt_hi_set")
        xt_lo_set = sem("xt_lo_set")
        q_done = sem("q_done")
        q_hi_set = sem("q_hi_set")
        q_lo_set = sem("q_lo_set")
        q_stored = sem("q_stored")
        ctx_loaded = sem("ctx_loaded")
        ct_turned = sem("ct_turned")
        ct_hi_set = sem("ct_hi_set")
        ct_lo_set = sem("ct_lo_set")
        k_done = sem("k_done")
        k_hi_set = sem("k_hi_set")
        k_lo_set = sem("k_lo_set")
        v_done = sem("v_done")
        v_set = sem("v_set")
        q_in = [[sem(f"q_in{h}{par}") for par in range(2)] for h in range(HALVES)]
        nat_done = sem("nat_done")
        max_done = sem("max_done")
        m_turned = sem("m_turned")
        m_neg = sem("m_neg")
        m_in = [sem("m_in0"), sem("m_in1")]
        st_done = sem("st_done")
        exp_done = sem("exp_done")
        pv_done = sem("pv_done")
        psum_added = sem("prob_sums")
        den_done = sem("den_done")
        den_copied = sem("den_copied")
        den_stored = sem("den_stored")
        den_in = sem("den_in")
        inv_set = sem("inv_set")
        inv_stored = sem("inv_stored")
        attn_set = sem("attn_set")
        attn_stored = [sem("attn_stored0"), sem("attn_stored1")]
        at_in = [sem("at_in0"), sem("at_in1")]
        res_in = [sem("res_in0"), sem("res_in1")]
        inv_in = [sem("inv_in0"), sem("inv_in1")]
        at_normal = sem("at_normal")
        at_hi_set = sem("at_hi_set")
        at_lo_set = sem("at_lo_set")
        o_done = sem("o_done")
        o_added = sem("o_added")
        out_stored = [sem("out_stored0"), sem("out_stored1")]

        block = stack.enter_context(nc.Block())

        x_rows = x.rearrange("b q n -> (b q) n")
        out_rows = out.rearrange("b q n -> (b q) n")

        def ct_bank(b, k):
            return NAT + k % 2 if isinstance(b, int) and b == 0 else TURN

        def q_bank(g, c):
            first = isinstance(g, int) and g == 0 and c in (2, 3)
            return CTX + c % 2 if first else DENSE + c % 2

        def natural(w):
            return w.rearrange("(k p) n -> k p n", p=P)

        W_ALL = [
            (Wq, Aq, Bq, H), (Wk, Ak, Bk, KVW), (Wv, Av, Bv, KVW), (Wo, Ao, Bo, H),
        ]
        W_O = 3
        FIRST_BLOCK = [0, KC, KC + 2, KC + 4, 2 * KC + 4]
        QKV_BLOCKS = FIRST_BLOCK[W_O]

        AB_LOADS = [16 * 5, 16 * 10, 16 * 15, 16 * (15 + NKV + 4)]
        RAW_LOADS = []
        for g in range(FIRST_BLOCK[4]):
            before = RAW_LOADS[g - 2] if g >= 2 else 0
            RAW_LOADS.append(before + 16 * (JH if g >= QKV_BLOCKS else 1))

        def lo_by_pool(g):
            return int(g % 2 == 1 and not KC <= g < QKV_BLOCKS)

        def lo_count(g):
            return sum(lo_by_pool(n) == lo_by_pool(g) for n in range(g + 1))

        def wait_lo(eng, g):
            eng.wait_ge(w_lo[lo_by_pool(g)], lo_count(g))

        def wait_qkv(eng):
            wait_lo(eng, QKV_BLOCKS - 1)
            wait_lo(eng, KC - 1)

        def w_block(w, n):
            if w == 0:
                return wq_hi[:, n, :], wq_lo[:, n, :]
            if w == W_O:
                return wo_hi[:, n, :], wo_lo[:, n, :]
            hi, lo = (wk_hi, wk_lo) if w == 1 else (wv_hi, wv_lo)
            return (t[:, 4 * n:4 * n + 4, :].rearrange("p k n -> p (k n)") for t in (hi, lo))

        def run_steps(eng, step, wo_factors):
            full = ({"A", "D", "V", "T", "N", "Q", "E1"}, {"A", "D", "G", "T", "K", "C", "N", "Q"})
            step(-1, 0, (set(), {"K", "C"}))
            step(-1, 1, ({"V", "T", "N", "E1"}, {"T", "K", "C", "N"}))
            wo_factors()
            step(0, 0, (full[0] - {"D"}, full[1] - {"G"}))
            with eng.Fori(0, (B - 4) // 2) as pair:
                step(pair, 1, full)
                step(pair, 2, full)
            step(B // 2 - 2, 1, (full[0], full[1] - {"C"}))
            step(B // 2 - 1, 0, ({"A", "D", "V", "N", "E1"}, {"A", "D", "G", "N", "W0"}))
            step(B // 2 - 1, 1, ({"A", "D", "W1"}, {"A", "D", "G", "W2"}))

        def store_den(eng, n, b, h):
            eng.wait_ge(den_copied, n + 1)
            eng.dma_start(den_scr[h * NN:(h + 1) * NN, bass.ds(b * NQ, NQ)].rearrange("(j r) q -> j r q", j=JH),
                          den_sb[0:P:HD, :].rearrange("j (r q) -> j r q", r=RH)).then_inc(den_stored, 16)

        def load_den(eng, b):
            eng.dma_start(den_rows[:, :], den_scr[:, bass.ds(b * NQ, NQ)]).then_inc(den_in, 16)

        def store_inv(eng, b):
            eng.wait_ge(inv_set, b + 1)
            eng.dma_start(inv_scr[:, bass.ds(b * NQ, NQ)], inv_rows[:, :]).then_inc(inv_stored, 16)

        @block.sync
        def _(sp):
            def load_ab(w):
                W, A, Bm, width = W_ALL[w]
                if w:
                    sp.wait_ge(a_placed, w)
                    sp.wait_ge(b_lo, w)
                if w == W_O:
                    heads = A.rearrange("(g r d) e -> g d r e", g=NKV, r=RH)
                    for g in range(NKV):
                        half, j = g // JH, g % JH
                        sp.dma_start(a_in[j * HD:(j + 1) * HD, half * RH:(half + 1) * RH, :], heads[g]
                                     ).then_inc(ab_in, 16)
                else:
                    sp.dma_start(a_in[:, :, :], A.rearrange("(k p) r -> p k r", p=P)).then_inc(ab_in, 16)
                for quad in range(4):
                    sp.dma_start(b_in[32 * quad:32 * quad + R, 0:width], Bm).then_inc(ab_in, 16)

            def load_raw(w, n):
                W = W_ALL[w][0]
                g = FIRST_BLOCK[w] + n
                raw = raw2 if w == W_O else raw1
                if g >= 2:
                    sp.wait_ge(w_summed, g - 1)
                if w == W_O:
                    half, r = n // RH, n % RH
                    for j in range(JH):
                        row = ((half * JH + j) * RH + r) * HD
                        sp.dma_start(raw[g % 2][j * HD:(j + 1) * HD, :], W[row:row + HD, :]).then_inc(raw_in[g % 2], 16)
                elif w == 0:
                    sp.dma_start(raw[g % 2][:, :], W[n * P:(n + 1) * P, :]).then_inc(raw_in[g % 2], 16)
                else:
                    sp.dma_start(raw[g % 2][:, :].rearrange("p (k n) -> p k n", k=4),
                                 W[n * 4 * P:(n + 1) * 4 * P, :].rearrange("(k p) n -> p k n", p=P)
                                 ).then_inc(raw_in[g % 2], 16)

            def load_x(g):
                sp.dma_start(x_in[:, :, :], x[bass.ds(g * QG, QG), :, :].rearrange("b q n -> q b n")
                             ).then_inc(x_loaded, 16)

            def load_ctx(b):
                sp.dma_start(ctx_in[:, :, :],
                             ctxt[bass.ds(b, 1), :, :].rearrange("b (t p) n -> p (b t) n", p=TR)
                             ).then_inc(ctx_loaded, 16)

            sp.wait_ge(zeroed, 1)
            load_ab(0)
            load_raw(0, 0)
            load_raw(0, 1)
            load_x(0)
            for n in range(2, KC):
                load_raw(0, n)
            load_ab(1)
            for n in range(2):
                load_raw(1, n)

            def store_q(g, half):
                sp.wait_ge(q_lo_set, g * 2 * RH + (half + 1) * RH)
                for hl, t in ((0, qev_hi), (1, qev_lo)):
                    sp.dma_start(q_scr[hl, bass.ds(g * QG, QG), half, :, :].rearrange("b p n -> p b n"),
                                 t[:, :, :, :].bitcast(F32).rearrange("p b r q -> p b (r q)")
                                 ).then_inc(q_stored, 16)

            def next_x(g):
                sp.wait_ge(xt_turned, (g + 1) * KC)
                load_x(g + 1)

            next_x(0)
            store_q(0, 0)
            load_ab(2)
            for n in range(2):
                load_raw(2, n)
            store_q(0, 1)
            load_ctx(0)
            load_ab(W_O)
            with sp.Fori(1, GROUPS - 1) as g:
                next_x(g)
                store_q(g, 0)
                store_q(g, 1)
            store_q(GROUPS - 1, 0)
            store_q(GROUPS - 1, 1)

            def load_q(pair, off, h):
                b = 2 * pair + off
                for n, hl in enumerate((0, 1, 0)):
                    sp.dma_start(qst[off % 2][32 * n:32 * n + HD, h * JH:(h + 1) * JH, :].bitcast(F32),
                                 q_scr[hl, bass.ds(b, 1), h, :, :].rearrange("b (j d) n -> d (b j) n", d=HD)
                                 ).then_inc(q_in[h][off % 2], 16)

            sp.wait_ge(q_stored, GROUPS * HALVES * 32)
            sp.wait_ge(q_done, GROUPS * 2 * RH)
            for off in range(2):
                for h in range(HALVES):
                    load_q(0, off, h)

            def store_attn(b, h):
                sp.wait_ge(attn_set, 2 * b + h + 1)
                sp.dma_start(at_scr[:, h * RH:(h + 1) * RH, bass.ds(b * NQ, NQ)], attn[h][:, :, :]
                             ).then_inc(attn_stored[h], 16)

            def load_inv(t, par):
                heads = inv_scr.rearrange("(h j r) n -> j h r n", h=HALVES, j=JH)
                for j in range(JH):
                    for h in range(HALVES):
                        sp.dma_start(inv[par][j * HD:(j + 1) * HD, h * RH:(h + 1) * RH, :],
                                     heads[j, h, :, bass.ds(t * P, P)].partition_broadcast(HD)
                                     ).then_inc(inv_in[par], 16)

            def load_attn(pair, par):
                t = 2 * pair + par
                if isinstance(pair, int) and pair == 0:
                    sp.wait_ge(st_done, 2 * NS * (B - 1 + par))
                    for h in range(HALVES):
                        sp.wait_ge(attn_stored[h], 16 * 3)
                    sp.wait_ge(inv_stored, 16 * 3)
                else:
                    sp.wait_ge(at_lo_set, t - 1)
                sp.dma_start(at_raw[par][:, :, :], at_scr[:, :, bass.ds(t * P, P)]).then_inc(at_in[par], 16)
                load_inv(t, par)

            def load_residual(pair, par):
                if not isinstance(pair, int) or pair > 0:
                    sp.wait_ge(out_stored[par], 16 * pair)
                sp.dma_start(res[par][:, :], x_rows[bass.ds((2 * pair + par) * P, P), :]).then_inc(res_in[par], 16)

            def store_tile(pair, par):
                t = 2 * pair + par
                sp.wait_ge(o_added, 2 * t + 2)
                sp.dma_start(out_rows[bass.ds(t * P, P), :], res[par][:, :]).then_inc(out_stored[par], 16)

            def step(pair, off, has):
                b = 2 * pair + off
                for h in range(HALVES):
                    if "W1" in has[h]:
                        load_attn(0, 0)
                        load_residual(0, 0)
                    for kind, i, k in half_order(h, has[h]):
                        if kind == "A":
                            store_attn(b - 1 + h, 1 - h)
                        elif kind == "D":
                            store_den(sp, 2 * b + h - 1, b - 1 + h, 1 - h)
                            if "G" in has[h]:
                                load_den(sp, b - 1)
                        elif kind == "J":
                            store_inv(sp, b - 1)
                        elif kind == "K" and i == 1 and k == 0 and "C" in has[h]:
                            sp.wait_ge(ct_turned, (b + 3) * KC)
                            load_ctx(b + 3)
                        elif kind == "M":
                            sp.wait_ge(m_neg, 2 * (b + 1) + h + 1)
                            sp.dma_start(qst[(off + 1) % 2][STK:STM, h * JH:(h + 1) * JH, :].bitcast(F32)
                                         .rearrange("p j (r q) -> p (j r) q", r=RH),
                                         neg_max[:, h, :].bitcast(F32)).then_inc(m_in[h], 16)
                        elif kind == "W" and i + 1 in range(2, KC):
                            load_raw(W_O, i + 1)
                        elif kind == "E" and "Q" in has[h]:
                            sp.wait_ge(st_done, NS * (2 * b + h + 1))
                            load_q(pair, off + 2, h)

            def wo_factors():
                load_raw(W_O, 0)
                load_raw(W_O, 1)

            run_steps(sp, step, wo_factors)
            load_attn(0, 1)
            load_residual(0, 1)
            store_attn(B - 1, 1)
            for h in range(HALVES):
                sp.wait_ge(attn_stored[h], 16 * B)
            sp.wait_ge(inv_stored, 16 * (B - 1))
            with sp.Fori(0, OT // 2 - 2) as pair:
                for par in range(2):
                    load_attn(pair + 1, par)
                    store_tile(pair, par)
                    load_residual(pair + 1, par)
            for par in range(2):
                if par == 1:
                    sp.wait_ge(inv_stored, 16 * B)
                load_attn(OT // 2 - 1, par)
                store_tile(OT // 2 - 2, par)
                load_residual(OT // 2 - 1, par)
            for par in range(2):
                store_tile(OT // 2 - 1, par)
            for par in range(2):
                sp.wait_ge(out_stored[par], 16 * (OT // 2))

        @block.gpsimd
        def _(pool):
            def pool_lo(w, n):
                g = FIRST_BLOCK[w] + n
                pool.wait_ge(w_hi, g + 1)
                hi, lo = w_block(w, n)
                pool.tensor_tensor(lo, (wsum2 if w == W_O else wsum1)[g % 2][:, :], hi, ALU.subtract
                                   ).then_inc(w_lo[1], 1)

            pool.memset(b_in[:, :], 0.0).then_inc(zeroed, 1)
            pool.memset(ident[:, :], 0.0).then_inc(ident_set, 1)
            pool.wait_ge(ident_set, 1)
            pool.affine_select(out=ident[:, :], in_=ident[:, :], compare_op=ALU.not_equal, fill=1.0, base=0,
                               pattern=[[-1, P]], channel_multiplier=1).then_inc(ident_set, 1)
            pool.memset(ones[:, :], 1.0).then_inc(ident_set, 1)
            for n in range(1, KC, 2):
                pool_lo(0, n)
            wait_qkv(pool)
            for par in range(2):
                pool.memset(kst[par][STK:STM, :, :].bitcast(F32), 1.0).then_inc(ones_row, 1)
                pool.wait_ge(ones_row, par + 1)
            pool.wait_ge(q_done, GROUPS * 2 * RH)
            for par, t in enumerate((ct_hi, ct_lo)):
                pool.memset(t[:, :, NT:NTE].bitcast(F32), 0.0).then_inc(ones_row, 1)
                pool.wait_ge(ones_row, par + 3)

            def step(pair, off, has):
                b = 2 * pair + off
                for h in range(HALVES):
                    n = 2 * b + h
                    for kind, i, k in half_order(h, has[h]):
                        if kind == "S" and i == 2 * JH - 1:
                            at_least(pool, den_done, n)
                            pool.wait_ge(exp_done, NS * n + 2 * JH)
                            pool.tensor_tensor(prob_sum[:, :, :], probs[:, 0, :, :], probs[:, 1, :, :], ALU.add
                                               ).then_inc(psum_added, 1)
                        elif kind == "S" and i == NS - 1:
                            pool.wait_ge(psum_added, 2 * n + 1)
                            pool.wait_ge(exp_done, NS * (n + 1))
                            pool.tensor_tensor(prob_sum[:, :, :], prob_sum[:, :, :], probs[:, 2, :, :], ALU.add
                                               ).then_inc(psum_added, 1)
                        elif kind == "W" and lo_by_pool(QKV_BLOCKS + i):
                            pool_lo(W_O, i)

            run_steps(pool, step, lambda: None)

        @block.tensor
        def _(pe):
            pe.wait_ge(ident_set, 3)

            def mm3(dst, l_hi, l_lo, r_hi, r_lo, start, stop):
                pe.matmul(dst, l_hi, r_hi, start=start, stop=False)
                pe.matmul(dst, l_hi, r_lo, start=False, stop=False)
                return pe.matmul(dst, l_lo, r_hi, start=False, stop=stop)

            def turn_a(w, bank):
                if w:
                    pe.wait_ge(w_summed, FIRST_BLOCK[w])
                pe.wait_ge(a_placed, w + 1)
                for k in range(KC):
                    mm = pe.transpose(ps[:, bank + k // 4, (k % 4) * P:(k % 4 + 1) * P],
                                      a_dup[:, k, :, :].rearrange("p a r -> p (a r)"), ident[:, :])
                mm.then_inc(a_turned, 1)

            def fold(w, n, bank):
                g = FIRST_BLOCK[w] + n
                width = W_ALL[w][3]
                a_st, b_st = (ast2, bst2) if w == W_O else (ast1, bst1)
                if n == 0:
                    pe.wait_ge(a_lo, w + 1)
                    pe.wait_ge(b_lo, w + 1)
                else:
                    pe.wait_ge(w_summed, g)
                for m in range(2):
                    if width == H:
                        mm = pe.matmul(ps[:, bank + m, :], a_st[:, n, :], b_st[:, m * BANK:(m + 1) * BANK],
                                       start=True, stop=True)
                    else:
                        for k in range(2):
                            mm = pe.matmul(ps[:, bank + m, k * KVW:(k + 1) * KVW], a_st[:, 4 * n + 2 * m + k, :],
                                           b_st[:, 0:KVW], start=True, stop=True)
                mm.then_inc(folded, 1)

            def turn_x(g, k):
                if k == 0:
                    pe.wait_ge(x_loaded, 16 * g + 16)
                at_least(pe, xt_lo_set, g * KC + k - 1)
                for b in range(QG):
                    mm = pe.transpose(ps[:, NAT + k % 2, b * NQ:(b + 1) * NQ], x_in[:, b, k * P:(k + 1) * P],
                                      ident[0:NQ, 0:NQ])
                mm.then_inc(xt_turned, 1)

            def q_piece(g, c, k):
                cols = slice(c * P, (c + 1) * P)
                return mm3(ps[:, q_bank(g, c), 0:QG * NQ], wq_hi[:, k, cols], wq_lo[:, k, cols],
                           xt_hi[:, k, :], xt_lo[:, k, :], k == 0, k == KC - 1)

            def q_chunk(g, c):
                if c >= 1:
                    pe.wait_ge(q_lo_set, g * 2 * RH + c - 1)
                for k in range(KC):
                    if c == 0:
                        pe.wait_ge(xt_lo_set, g * KC + k + 1)
                    mm = q_piece(g, c, k)
                    if c == 2 * RH - 1:
                        if k == KC - 1:
                            mm.then_inc(q_done, 1)
                        if isinstance(g, int) and g == GROUPS - 1:
                            turn_ctx(0, k)
                        else:
                            turn_x(g + 1, k)
                if c < 2 * RH - 1:
                    mm.then_inc(q_done, 1)

            def turn_ctx(b, k):
                if k == 0:
                    pe.wait_ge(ctx_loaded, 16 * (b + 1))
                bank = ct_bank(b, k)
                if bank != TURN:
                    at_least(pe, ct_lo_set, k - 1)
                elif k == 0:
                    pe.wait_ge(k_lo_set, NKV * b)
                else:
                    pe.wait_ge(ct_lo_set, b * KC + k)
                for t in range(TC):
                    mm = pe.transpose(ps[:, bank, t * TR:(t + 1) * TR], ctx_in[:, t, k * P:(k + 1) * P],
                                      ident[0:TR, 0:TR])
                mm.then_inc(ct_turned, 1)

            def q_first(k):
                wait_lo(pe, k)
                pe.wait_ge(xt_lo_set, k + 1)
                for c in range(4):
                    mm = q_piece(0, c, k)
                    if k == KC - 1:
                        mm.then_inc(q_done, 1)

            turn_a(0, FOLD)
            for k in range(KC):
                turn_x(0, k)
                fold(0, k, FOLD)
                if k:
                    q_first(k - 1)
            q_first(KC - 1)
            turn_a(1, FOLD)
            q_chunk(0, 4)
            fold(1, 0, FOLD)
            q_chunk(0, 5)
            fold(1, 1, FOLD)
            turn_a(2, FOLD)
            q_chunk(0, 6)
            fold(2, 0, FOLD)
            q_chunk(0, 7)
            fold(2, 1, FOLD)
            pe.wait_ge(q_lo_set, 2 * RH - 1)
            with pe.Fori(1, GROUPS - 1) as g:
                for c in range(2 * RH):
                    q_chunk(g, c)
                pe.wait_ge(q_lo_set, g * 2 * RH + 2 * RH - 1)
            for c in range(2 * RH):
                q_chunk(GROUPS - 1, c)
            pe.wait_ge(q_lo_set, GROUPS * 2 * RH)
            wait_qkv(pe)
            pe.wait_ge(ones_row, 4)

            def step(pair, off, has):
                b = 2 * pair + off
                cur, nxt = off % 2, (off + 1) % 2
                for h in range(HALVES):
                    n = 2 * b + h
                    m = 2 * (b + 1) + h
                    for kind, i, k in half_order(h, has[h]):
                        if kind == "V":
                            if k == 0 and i == 0:
                                at_least(pe, k_lo_set, NKV * (b + 1) + JH)
                            dst = ps[0:TR, VA + i // 2, (i % 2) * KVW:(i % 2 + 1) * KVW]
                            rows = slice(i * TR, (i + 1) * TR)
                            pe.matmul(dst, ct_hi[:, k, rows], wv_hi[:, k, :], start=(k == 0 and i != 1), stop=False,
                                      skip_group_check=True)
                            pe.matmul(dst, ct_hi[:, k, rows], wv_lo[:, k, :], start=False, stop=False,
                                      skip_group_check=True)
                            mm = pe.matmul(dst, ct_lo[:, k, rows], wv_hi[:, k, :], start=False,
                                           stop=(k == KC - 1), skip_group_check=True)
                            if k == KC - 1 and i >= 1:
                                mm.then_inc(v_done, 1)
                        elif kind == "T":
                            turn_ctx(b + 2, i)
                        elif kind == "K":
                            if k == 0:
                                at_least(pe, v_set, 2 * (b + 1) + 2)
                                if i == 1:
                                    pe.wait_ge(ct_lo_set, (b + 3) * KC)
                            if i == 0:
                                pe.wait_ge(ct_lo_set, (b + 2) * KC + k + 1)
                            cols = slice(i * P, (i + 1) * P)
                            mm = mm3(ps[:, (VA, TURN)[i], 0:NTE], wk_hi[:, k, cols], wk_lo[:, k, cols],
                                     ct_hi[:, k, :], ct_lo[:, k, :], k == 0, k == KC - 1)
                            if k == KC - 1:
                                mm.then_inc(k_done, 1)
                        elif kind == "S":
                            if i == 0:
                                pe.wait_ge(m_in[h], 16 * (b + 1))
                            same = [s for s in range(i) if score_bank(s) == score_bank(i)]
                            if i == 0:
                                at_least(pe, exp_done, NS * n - 1)
                            elif i == S_IN_DEN[0]:
                                at_least(pe, den_copied, n)
                            else:
                                pe.wait_ge(exp_done, NS * n + same[-1] + 1)
                            if i == S_IN_DEN[0] and isinstance(n, int) and n == 0:
                                pe.wait_ge(a_lo, W_O + 1)
                            g, c = h * JH + i % JH, i // JH
                            pe.matmul(ps[0:TR, score_bank(i), 0:QH], kst[cur][0:STM, g, c * TR:(c + 1) * TR],
                                      qst[cur][0:STM, g, :], start=True, stop=True).then_inc(st_done, 1)
                        elif kind == "N":
                            if i == 0:
                                pe.wait_ge(q_in[h][nxt], 48 * (pair + (off + 1) // 2 + 1))
                                pe.wait_ge(k_lo_set, JH * (m + 1))
                                at_least(pe, m_neg, m)
                            at_least(pe, max_done, NN * m + i - 1)
                            g, rr = h * JH + i // RH, i % RH
                            mm = pe.matmul(ps[0:NQ, NAT + i % 2, 0:NTE], qst[nxt][0:STK, g, rr * NQ:(rr + 1) * NQ],
                                           kst[nxt][0:STK, g, :], start=True, stop=True)
                            mm.then_inc(nat_done, 1)
                        elif kind == "M":
                            pe.wait_ge(max_done, NN * (m + 1))
                            pe.transpose(ps[0:JH * RH, NAT, 0:NQ], maxima[:, h, :], ident[0:NQ, 0:NQ]
                                         ).then_inc(m_turned, 1)
                        elif kind == "P":
                            pe.wait_ge(exp_done, NS * n + JH * (i + 1))
                            if i == 0:
                                at_least(pe, attn_set, n)
                                pe.wait_ge(v_set, 2 * (b + 1))
                            for j in range(JH):
                                g = h * JH + j
                                mm = pe.matmul(ps[HD * j:HD * (j + 1), CTX, 0:QH],
                                               v_sb[cur][:, i, g * HD:(g + 1) * HD], probs[:, i, j, :],
                                               start=(i == 0), stop=(i == TC - 1))
                            mm.then_inc(pv_done, 1)
                        elif kind == "D":
                            denominators(n - 1)
                        elif kind == "W":
                            if i == 0:
                                pe.wait_ge(v_set, 2 * B)
                            fold(W_O, i, FOLD_O)
                        elif kind == "O":
                            if i == 0:
                                pe.wait_ge(at_lo_set, 1)
                                pe.wait_ge(m_neg, 2 * B)
                            wait_lo(pe, QKV_BLOCKS + i)
                            for m in range(2):
                                o_piece(0, m, i, NAT).then_inc(o_done, 1) if i == KC - 1 else o_piece(0, m, i, NAT)

            def o_piece(par, m, k, bank):
                cols = slice(m * BANK, (m + 1) * BANK)
                return mm3(ps[:, bank + m, :], at_hi[par][:, k, :], at_lo[par][:, k, :],
                           wo_hi[:, k, cols], wo_lo[:, k, cols], k == 0, k == KC - 1)

            def denominators(n):
                pe.wait_ge(psum_added, 2 * n + 2)
                for j in range(JH):
                    mm = pe.matmul(ps[HD * j:HD * (j + 1), DEN, 0:QH], ones[:, :], prob_sum[:, j, :],
                                   start=True, stop=True)
                mm.then_inc(den_done, 1)

            def wo_factors():
                turn_a(W_O, CTX)

            run_steps(pe, step, wo_factors)
            denominators(2 * B - 1)

            def tile(pair, par):
                t = 2 * pair + par
                pe.wait_ge(at_lo_set, t + 1)
                for m in range(2):
                    at_least(pe, o_added, 2 * t + m - 1)
                    for k in range(KC):
                        mm = o_piece(par, m, k, DENSE)
                    mm.then_inc(o_done, 1)

            wait_lo(pe, FIRST_BLOCK[4] - 1)
            tile(0, 1)
            with pe.Fori(1, OT // 2) as pair:
                tile(pair, 0)
                tile(pair, 1)

        @block.scalar
        def _(act):
            def ab_hi(w, bank):
                a_st, b_st = (ast2, bst2) if w == W_O else (ast1, bst1)
                width = W_ALL[w][3]
                act.wait_ge(ab_in, AB_LOADS[w])
                at_least(act, folded, FIRST_BLOCK[w])
                act.activation(b_st[:, 0:width], b_in[:, 0:width], ACT.Copy).then_inc(b_hi, 1)
                act.wait_ge(a_turned, w + 1)
                act.activation(a_st[:, :, :].rearrange("p k n -> p (k n)"),
                               ps[:, bank:bank + 2, :].rearrange("p a n -> p (a n)"), ACT.Copy, scale=LORA
                               ).then_inc(a_hi, 1)

            def block_hi(w, n):
                g = FIRST_BLOCK[w] + n
                act.wait_ge(w_summed, g + 1)
                hi, lo = w_block(w, n)
                act.activation(hi, (wsum2 if w == W_O else wsum1)[g % 2][:, :], ACT.Copy).then_inc(w_hi, 1)

            def x_hi(g, k):
                act.wait_ge(xt_turned, g * KC + k + 1)
                act.activation(xt_hi[:, k, :], ps[:, NAT + k % 2, 0:QG * NQ], ACT.Copy).then_inc(xt_hi_set, 1)

            def q_hi(g, c):
                if c % RH == 0:
                    at_least(act, q_stored, 32 * (2 * g + c // RH))
                act.wait_ge(q_done, g * 2 * RH + c + 1)
                act.activation(qev_hi[:, :, c % RH, :],
                               ps[:, q_bank(g, c), 0:QG * NQ].rearrange("p (b q) -> p b q", b=QG), ACT.Copy
                               ).then_inc(q_hi_set, 1)

            def ctx_hi(b, k):
                act.wait_ge(ct_turned, b * KC + k + 1)
                act.activation(ct_hi[:, k, 0:NT], ps[:, ct_bank(b, k), 0:NT], ACT.Copy).then_inc(ct_hi_set, 1)

            def k_hi(b, par, half, j):
                act.wait_ge(k_done, 2 * b + half + 1)
                at_least(act, st_done, NS * (2 * (b - 2) + half + 1))
                for quad in range(2):
                    op = act.activation(kst[par][HD * quad:HD * (quad + 1), half * JH + j, :],
                                        ps[HD * j:HD * (j + 1), (VA, TURN)[half], 0:NTE], ACT.Copy)
                op.then_inc(k_hi_set, 1)

            ab_hi(0, FOLD)
            for k in range(KC):
                x_hi(0, k)
                block_hi(0, k)
            ab_hi(1, FOLD)
            for c in range(4):
                q_hi(0, c)
            q_hi(0, 4)
            block_hi(1, 0)
            q_hi(0, 5)
            block_hi(1, 1)
            ab_hi(2, FOLD)
            q_hi(0, 6)
            block_hi(2, 0)
            for k in range(KC):
                x_hi(1, k)
            q_hi(0, 7)
            block_hi(2, 1)
            with act.Fori(1, GROUPS - 1) as g:
                for c in range(2 * RH - 1):
                    q_hi(g, c)
                for k in range(KC):
                    x_hi(g + 1, k)
                q_hi(g, 2 * RH - 1)
            for c in range(2 * RH - 1):
                q_hi(GROUPS - 1, c)
            for k in range(KC):
                ctx_hi(0, k)
            q_hi(GROUPS - 1, 2 * RH - 1)

            def step(pair, off, has):
                b = 2 * pair + off
                cur, nxt = off % 2, (off + 1) % 2
                for h in range(HALVES):
                    n = 2 * b + h
                    m = 2 * (b + 1) + h
                    for kind, i, k in half_order(h, has[h]):
                        if kind == "V" and k == KC - 1 and i >= 1:
                            act.wait_ge(v_done, 2 * (b + 1) + i)
                            wide = 2 * KVW if i == 1 else KVW
                            c0 = 0 if i == 1 else 2
                            act.activation(v_sb[nxt][:, c0:i + 1, :].rearrange("p c n -> p (c n)"),
                                           ps[0:TR, VA + i // 2, 0:wide], ACT.Copy).then_inc(v_set, 1)
                        elif kind == "T":
                            ctx_hi(b + 2, i)
                        elif kind == "E0":
                            k_hi(b + 2, cur, 0, i)
                        elif kind == "E1":
                            k_hi(b + 1, nxt, 1, i)
                        elif kind == "S":
                            c, j = i // JH, i % JH
                            act.wait_ge(st_done, NS * n + i + 1)
                            at_least(act, pv_done, 3 * n + c - 2)
                            at_least(act, psum_added, 2 * n - (1 if c < 2 else 0))
                            act.activation(probs[:, c, j, :], ps[0:TR, score_bank(i), 0:QH], ACT.Exp, scale=SM
                                           ).then_inc(exp_done, 1)
                        elif kind == "D":
                            copy_den(n - 1)
                        elif kind == "M":
                            act.wait_ge(m_turned, m + 1)
                            at_least(act, m_in[h], 16 * (b + 1))
                            act.activation(neg_max[:, h, :], ps[0:JH * RH, NAT, 0:NQ], ACT.Copy, scale=-1.0
                                           ).then_inc(m_neg, 1)
                        elif kind == "W":
                            block_hi(W_O, i)
                        elif kind == "O" and i == 0:
                            split(0, 0)

            def copy_den(n):
                act.wait_ge(den_done, n + 1)
                at_least(act, den_stored, 16 * n)
                act.activation(den_sb[:, :], ps[:, DEN, 0:QH], ACT.Copy).then_inc(den_copied, 1)

            def split(pair, par):
                t = 2 * pair + par
                act.wait_ge(at_normal, t + 1)
                at_least(act, o_done, 2 * (t - 1))
                act.activation(at_hi[par][:, :, :], at_raw[par][:, :, :], ACT.Copy).then_inc(at_hi_set, 1)

            def wo_factors():
                act.wait_ge(q_stored, GROUPS * HALVES * 32)
                ab_hi(W_O, CTX)

            run_steps(act, step, wo_factors)
            copy_den(2 * B - 1)
            store_den(act, 2 * B - 1, B - 1, 1)
            split(0, 1)
            act.wait_ge(den_stored, 16 * 2 * B)
            load_den(act, B - 1)
            store_inv(act, B - 1)
            with act.Fori(1, OT // 2) as pair:
                split(pair, 0)
                split(pair, 1)

        @block.vector
        def _(dve):
            dve.memset(a_dup[:, :, :, :].rearrange("p k a r -> p (k a r)"), 0.0).then_inc(a_placed_pad, 1)
            dve.wait_ge(a_placed_pad, 1)

            def ab_place(w):
                dve.wait_ge(ab_in, AB_LOADS[w])
                at_least(dve, a_turned, w)
                for quad in range(4):
                    op = dve.tensor_copy(a_dup[:, :, quad, 0:R], a_in[:, :, :])
                op.then_inc(a_placed, 1)

            def ab_lo(w, bank):
                a_st, b_st = (ast2, bst2) if w == W_O else (ast1, bst1)
                width = W_ALL[w][3]
                dve.wait_ge(b_hi, w + 1)
                dve.tensor_tensor(b_st[64:128, 0:width], b_in[64:128, 0:width], b_st[64:128, 0:width], ALU.subtract
                                  ).then_inc(b_lo, 1)
                dve.wait_ge(a_hi, w + 1)
                for quad in (1, 3):
                    rows = slice(32 * quad, 32 * quad + 32)
                    st = a_st[rows, :, :].rearrange("p k n -> p (k n)")
                    op = dve.scalar_tensor_tensor(out=st, in0=ps[rows, bank:bank + 2, :].rearrange("p a n -> p (a n)"),
                                                  scalar=LORA, in1=st, op0=ALU.mult, op1=ALU.subtract)
                op.then_inc(a_lo, 1)

            def block_sum(w, n, bank):
                g = FIRST_BLOCK[w] + n
                raw, wsum = (raw2, wsum2) if w == W_O else (raw1, wsum1)
                dve.wait_ge(folded, g + 1)
                dve.wait_ge(raw_in[g % 2], RAW_LOADS[g])
                if g >= 2:
                    wait_lo(dve, g - 2)
                if w == 0:
                    for m in range(2):
                        cols = slice(m * BANK, (m + 1) * BANK)
                        op = dve.tensor_tensor(
                            wsum[g % 2][:, cols].rearrange("p (r j d) -> p j r d", r=RH, j=JH),
                            ps[:, bank + m, :].rearrange("p (j r d) -> p j r d", j=JH, r=RH),
                            raw[g % 2][:, cols].rearrange("p (j r d) -> p j r d", j=JH, r=RH), ALU.add)
                else:
                    op = dve.tensor_tensor(wsum[g % 2][:, :], ps[:, bank:bank + 2, :].rearrange("p a n -> p (a n)"),
                                           raw[g % 2][:, :], ALU.add)
                op.then_inc(w_summed, 1)

            def block_lo(w, n):
                g = FIRST_BLOCK[w] + n
                if lo_by_pool(g):
                    return
                dve.wait_ge(w_hi, g + 1)
                hi, lo = w_block(w, n)
                dve.tensor_tensor(lo, (wsum2 if w == W_O else wsum1)[g % 2][:, :], hi, ALU.subtract
                                  ).then_inc(w_lo[0], 1)

            def x_lo(g, k):
                dve.wait_ge(xt_hi_set, g * KC + k + 1)
                dve.tensor_tensor(xt_lo[:, k, :], ps[:, NAT + k % 2, 0:QG * NQ], xt_hi[:, k, :], ALU.subtract
                                  ).then_inc(xt_lo_set, 1)

            def q_lo(g, c):
                dve.wait_ge(q_hi_set, g * 2 * RH + c + 1)
                dve.tensor_tensor(qev_lo[:, :, c % RH, :],
                                  ps[:, q_bank(g, c), 0:QG * NQ].rearrange("p (b q) -> p b q", b=QG),
                                  qev_hi[:, :, c % RH, :], ALU.subtract).then_inc(q_lo_set, 1)

            def ctx_lo(b, k):
                dve.wait_ge(ct_hi_set, b * KC + k + 1)
                dve.tensor_tensor(ct_lo[:, k, 0:NT], ps[:, ct_bank(b, k), 0:NT], ct_hi[:, k, 0:NT], ALU.subtract
                                  ).then_inc(ct_lo_set, 1)

            def k_lo(b, par, half, j):
                dve.wait_ge(k_hi_set, NKV * b + half * JH + j + 1)
                dve.tensor_tensor(kst[par][2 * HD:3 * HD, half * JH + j, :],
                                  ps[HD * j:HD * (j + 1), (VA, TURN)[half], 0:NTE],
                                  kst[par][0:HD, half * JH + j, :], ALU.subtract).then_inc(k_lo_set, 1)

            ab_place(0)
            ab_lo(0, FOLD)
            for k in range(KC):
                x_lo(0, k)
                block_sum(0, k, FOLD)
                if k:
                    block_lo(0, k - 1)
            block_lo(0, KC - 1)
            ab_place(1)
            ab_lo(1, FOLD)
            for c in range(5):
                q_lo(0, c)
            block_sum(1, 0, FOLD)
            block_lo(1, 0)
            q_lo(0, 5)
            block_sum(1, 1, FOLD)
            block_lo(1, 1)
            ab_place(2)
            ab_lo(2, FOLD)
            q_lo(0, 6)
            block_sum(2, 0, FOLD)
            block_lo(2, 0)
            for k in range(KC):
                x_lo(1, k)
            q_lo(0, 7)
            block_sum(2, 1, FOLD)
            block_lo(2, 1)
            with dve.Fori(1, GROUPS - 1) as g:
                for c in range(2 * RH - 1):
                    q_lo(g, c)
                for k in range(KC):
                    x_lo(g + 1, k)
                q_lo(g, 2 * RH - 1)
            for c in range(2 * RH - 1):
                q_lo(GROUPS - 1, c)
            for k in range(KC):
                ctx_lo(0, k)
            q_lo(GROUPS - 1, 2 * RH - 1)
            ab_place(W_O)

            def invert(b):
                dve.wait_ge(den_in, 16 * (b + 1))
                at_least(dve, inv_stored, 16 * b)
                dve.reciprocal(inv_rows[:, :], den_rows[:, :]).then_inc(inv_set, 1)

            def copy_attn(b, n, h):
                dve.wait_ge(pv_done, TC * (n + 1))
                at_least(dve, attn_stored[h], 16 * b)
                dve.tensor_copy(attn[h][:, :, :].rearrange("p r q -> p (r q)"), ps[:, CTX, 0:QH]
                                ).then_inc(attn_set, 1)

            def step(pair, off, has):
                b = 2 * pair + off
                cur = off % 2
                for h in range(HALVES):
                    n = 2 * b + h
                    m = 2 * (b + 1) + h
                    for kind, i, k in half_order(h, has[h]):
                        if kind == "T":
                            ctx_lo(b + 2, i)
                        elif kind == "E0":
                            k_lo(b + 2, cur, 0, i)
                        elif kind == "E1":
                            k_lo(b + 1, (off + 1) % 2, 1, i)
                        elif kind == "N":
                            dve.wait_ge(nat_done, NN * m + i + 1)
                            dve.tensor_reduce(maxima[:, h, i:i + 1], ps[0:NQ, NAT + i % 2, 0:NT], AX.X,
                                              ALU.max).then_inc(max_done, 1)
                        elif kind == "I":
                            invert(b - 1)
                        elif kind == "A":
                            copy_attn(b - 1 + h, n - 1, 1 - h)
                        elif kind == "W":
                            block_sum(W_O, i, FOLD_O)
                            block_lo(W_O, i)
                        elif kind == "O" and i == 0:
                            normalise(0, 0)
                            split(0, 0)

            def normalise(pair, par):
                dve.wait_ge(at_in[par], 16 * (pair + 1))
                dve.wait_ge(inv_in[par], 16 * NKV * (pair + 1))
                dve.tensor_tensor(at_raw[par][:, :, :], at_raw[par][:, :, :], inv[par][:, :, :], ALU.mult
                                  ).then_inc(at_normal, 1)

            def split(pair, par):
                dve.wait_ge(at_hi_set, 2 * pair + par + 1)
                dve.tensor_tensor(at_lo[par][:, :, :], at_raw[par][:, :, :], at_hi[par][:, :, :], ALU.subtract
                                  ).then_inc(at_lo_set, 1)

            def add_residual(pair, par):
                t = 2 * pair + par
                dve.wait_ge(res_in[par], 16 * (pair + 1))
                for m in range(2):
                    dve.wait_ge(o_done, 2 * t + m + 1)
                    part = res[par][:, m * BANK:(m + 1) * BANK]
                    bank = NAT if isinstance(pair, int) and t == 0 else DENSE
                    dve.tensor_tensor(part, ps[:, bank + m, :], part, ALU.add).then_inc(o_added, 1)

            def wo_factors():
                ab_lo(W_O, CTX)

            run_steps(dve, step, wo_factors)
            copy_attn(B - 1, 2 * B - 1, 1)
            normalise(0, 1)
            split(0, 1)
            invert(B - 1)
            for par in range(2):
                normalise(1, par)
                add_residual(0, par)
                split(1, par)
            with dve.Fori(1, OT // 2 - 1) as pair:
                for par in range(2):
                    normalise(pair + 1, par)
                    add_residual(pair, par)
                    split(pair + 1, par)
            for par in range(2):
                add_residual(OT // 2 - 1, par)


_INS = ['x', 'ctx_4096', 'L0_xattn_Wq', 'L0_xattn_Aq', 'L0_xattn_Bq', 'L0_xattn_Wk', 'L0_xattn_Ak', 'L0_xattn_Bk',
        'L0_xattn_Wv', 'L0_xattn_Av', 'L0_xattn_Bv', 'L0_xattn_Wo', 'L0_xattn_Ao', 'L0_xattn_Bo']
_OUTS = [((B, NQ, H), 'float32')]


def kernel(**inputs):
    import numpy as _np
    import concourse.bacc as _bacc
    from concourse import mybir as _mybir
    from concourse.bass_utils import run_bass_kernel_spmd as _run

    nc = _bacc.Bacc("TRN2", target_bir_lowering=False, num_devices=1)
    arrays, args = {}, []
    for name in _INS:
        a = _np.ascontiguousarray(inputs[name])
        arrays[f"in_{name}_dram"] = a
        args.append(nc.dram_tensor(f"in_{name}_dram", a.shape, _mybir.dt.from_np(a.dtype), kind="ExternalInput").ap())
    for i, (shape, dtype) in enumerate(_OUTS):
        dt = _mybir.dt.from_np(_np.dtype(dtype))
        args.append(nc.dram_tensor(f"out_{i}_dram", shape, dt, kind="ExternalOutput").ap())
    xattn_kernel(nc, *args)
    r = _run(nc, [arrays], core_ids=[0])
    return r.results[0]["out_0_dram"]
```

```python
from contextlib import ExitStack

import concourse.bass as bass
from concourse import mybir

ALU = mybir.AluOpType
ACT = mybir.ActivationFunctionType
AX = mybir.AxisListType
F32 = mybir.dt.float32
F32R = mybir.dt.float32r

B, NQ, H = 16, 112, 1024
NT = 375
NH, NKV, HD = 32, 8, 32
R = 16
LORA = 32.0 / 16.0
P = 128
KC = H // P
HALVES = 2
JH = NKV // HALVES
RH = NH // NKV
QH = RH * NQ
KVW = NKV * HD
TC = 3
TR = NT // TC
NTE = NT + 1
QG = 4
GROUPS = B // QG
QS = 4
SM = 1.0 / float(HD) ** 0.5
ROWS = B * NQ
OT = ROWS // P
BANK = 512
WBLK = H
assert TR * TC == NT and QH <= BANK and OT * P == ROWS and GROUPS * QG == B

STK = 3 * HD
NS = TC * JH
NN = JH * RH
STM = STK + 1

NAT = 0
STB = 2
TURN = 3
VA, VB = 4, 5
CTX = 6
DEN = 7
S_IN_DEN = (3, 5, 7, 9, 11)
FOLD = 2
FOLD_O = 4
DENSE = 4
OUT = (6, 4)

PLAN = sorted(
    [("S", i, 0.01 + 0.07 * i) for i in range(TC * JH)]
    + [("P", 0, 0.31), ("P", 1, 0.583), ("P", 2, 0.925), ("A", 0, 0.048), ("D", 0, 0.097)]
    + [("I", 0, 0.35), ("J", 0, 0.45)]
    + [("N", i, 0.03 + 0.052 * i) for i in range(JH * RH)] + [("M", 0, 0.925)]
    + [("E0", j, 0.62 + 0.08 * j) for j in range(JH)] + [("E1", j, 0.03 + 0.06 * j) for j in range(JH)]
    + [("F0", j, 0.62 + 0.08 * j) for j in range(JH)] + [("F1", j, 0.03 + 0.06 * j) for j in range(JH)],
    key=lambda item: item[2])
COST = {"S": QH, "P": 4 * QH, "D": 4 * QH, "N": NTE, "M": 2 * NQ, "V": 3 * KVW, "T": 2 * NT, "K": 2.7 * NTE,
        "W": 2 * BANK, "O": 6 * BANK, "Z": 3 * BANK}
LAG = 3
OLAG = 4


def half_order(h, has):
    dense = []
    if h == 0:
        for k in range(KC):
            dense += [("V", t, k) for t in range(TC) if "V" in has]
            dense += [("T", k - LAG, 0)] if "T" in has and k >= LAG else []
    if h == 1:
        for k in range(KC):
            dense += [("K", 0, k)] if "K" in has else []
            dense += [("T", KC - LAG + k // 2, 0)] if "T" in has and k % 2 == 0 and k // 2 < LAG else []
        dense += [("K", 1, k) for k in range(KC) if "K" in has]
    for name, first in (("W0", 0), ("W1", 4), ("W2", 8)):
        if name in has:
            for n in range(first, first + 4 if name != "W2" else KC + OLAG):
                dense += [("W", n, 0)] if n < KC else []
                dense += [("O", n - OLAG, 0)] if OLAG <= n < KC + OLAG else []
    if "W2" in has:
        dense += [("Z", m, k) for m in range(2) for k in range(KC)]
    need = {"S": "A", "P": "A", "D": "D", "A": "D", "I": "G", "J": "G", "N": "N", "M": "N",
            "E0": "K", "F0": "K", "E1": "E1", "F1": "E1"}
    plan = [item for item in PLAN if need[item[0]] in has]
    order, at = [], 0
    total = sum(COST.get(piece[0], 0) for piece in dense + plan)
    for piece in dense:
        while plan and plan[0][2] * total <= at:
            order.append((plan[0][0], plan[0][1], 0))
            at += COST.get(plan.pop(0)[0], 0)
        order.append(piece)
        at += COST[piece[0]]
    order += [(kind, i, 0) for kind, i, _ in plan]
    assert "K" not in has or order.index(("K", 0, KC - 1)) < order.index(("E0", 0, 0))
    return order + [("E", 0, 0)]


def score_bank(i):
    return DEN if i in S_IN_DEN else STB


def at_least(eng, sem, n):
    if not isinstance(n, int) or n > 0:
        eng.wait_ge(sem, n)


def xattn_kernel(nc, x, ctxt, Wq, Aq, Bq, Wk, Ak, Bk, Wv, Av, Bv, Wo, Ao, Bo, out):
    stack = ExitStack()
    with stack:
        base = (nc.sbuf_base + 31) // 32 * 32
        limit = nc.sbuf_usable_end
        top = [base]

        def region(size):
            at = top[0]
            top[0] += (size + 31) // 32 * 32
            assert top[0] <= limit, (top[0], limit)
            return at

        def place(name, shape, dt, at):
            n = 4
            for s in shape[1:]:
                n *= s
            return nc.alloc_sbuf_tensor_at(name, shape, dt, offset=at), at + (n + 31) // 32 * 32

        r_small = region(512 + 128 + 128 + 2 * NQ * 4 + 512)
        r_ab = region(2 * 4 * H)
        r_w = region(2 * KC * H * 4)
        r_kv = region(4 * KC * KVW * 4)
        r_ct = region(2 * KC * QG * NQ * 4)
        r_cin = region(TC * H * 4)
        r_ks = region(2 * NKV * NTE * 4)
        r_v = region(2 * TC * KVW * 4)
        r_x = region(QG * H * 4 + 2 * QG * QH * 4)

        at = r_small
        ident, at = place("ident", [P, P], F32, at)
        ones, at = place("ones", [TR, HD], F32, at)
        maxima, at = place("maxima", [NQ, HALVES, JH * RH], F32, at)
        neg_max, at = place("neg_max", [JH * RH, HALVES, NQ], F32R, at)
        a_in, at = place("a_in", [P, KC, R], F32, at)
        a_dup, at = place("a_dup", [P, KC, 4, 32], F32, r_ab)
        b_in, at = place("b_in", [P, H], F32, at)

        wq_hi, at = place("wq_hi", [P, KC, H], F32R, r_w)
        wq_lo, at = place("wq_lo", [P, KC, H], F32R, at)
        at = r_w
        qst = [None, None]
        for par in range(2):
            qst[par], at = place(f"q_stack{par}", [P, NKV, QH], F32R, at)
        probs, at = place("probs", [TR, TC, JH, QH], F32, at)
        prob_sum, at = place("prob_sum", [TR, JH, QH], F32, at)
        den_sb, at = place("denominators", [P, QH], F32, at)
        den_rows, at = place("den_rows", [NH, NQ], F32, at)
        inv_rows, at = place("inv_rows", [NH, NQ], F32, at)
        attn = [None, None]
        for h in range(HALVES):
            attn[h], at = place(f"attn{h}", [P, RH, NQ], F32, at)
        assert at <= r_kv

        wk_hi, at = place("wk_hi", [P, KC, KVW], F32R, r_kv)
        wk_lo, at = place("wk_lo", [P, KC, KVW], F32R, at)
        wv_hi, at = place("wv_hi", [P, KC, KVW], F32R, at)
        wv_lo, at = place("wv_lo", [P, KC, KVW], F32R, at)
        xt_hi, at = place("xt_hi", [P, KC, QG * NQ], F32R, r_ct)
        xt_lo, at = place("xt_lo", [P, KC, QG * NQ], F32R, at)
        ct_hi, at = place("ct_hi", [P, KC, NTE], F32R, r_ct)
        ct_lo, at = place("ct_lo", [P, KC, NTE], F32R, r_ct + KC * QG * NQ * 4)
        ctx_in, at = place("ctx_in", [TR, TC, H], F32, r_cin)
        wo_hi, at = place("wo_hi", [P, KC, H], F32R, r_kv)
        wo_lo, at = place("wo_lo", [P, KC, H], F32R, r_ct)
        assert at <= r_ks

        kst, v_sb = [None, None], [None, None]
        at = r_ks
        for par in range(2):
            kst[par], at = place(f"k_stack{par}", [P, NKV, NTE], F32R, at)
        at = r_v
        for par in range(2):
            v_sb[par], at = place(f"v{par}", [TR, TC, KVW], F32, at)
        x_in, at = place("x_in", [NQ, QG, H], F32, r_x)
        qev_hi, at = place("q_out_hi", [P, QG, RH, NQ], F32R, at)
        qev_lo, at = place("q_out_lo", [P, QG, RH, NQ], F32R, at)

        def staging(tag, at):
            raw = [None, None]
            wsum = [None, None]
            for par in range(2):
                raw[par], at = place(f"w_raw{tag}{par}", [P, WBLK], F32, at)
                wsum[par], at = place(f"w_sum{tag}{par}", [P, WBLK], F32, at)
            a_st, at = place(f"a_stack{tag}", [P, KC, P], F32R, at)
            b_st, at = place(f"b_stack{tag}", [P, H], F32R, at)
            return raw, wsum, a_st, b_st, at

        raw1, wsum1, ast1, bst1, at = staging("_qkv", r_ks)
        assert at <= r_x
        raw2, wsum2, ast2, bst2, at = staging("_o", r_x)
        assert at <= top[0]

        at_raw, at_hi, at_lo, inv, res = ([None, None] for _ in range(5))
        at_raw[0], at = place("attn_rows0", [P, KC, P], F32, r_ab)
        inv[0], at = place("inv_tile0", [P, KC, P], F32, at)
        assert at <= r_w
        at_hi[0], at = place("attn_hi0", [P, KC, P], F32R, max(r_cin, r_ct + KC * H * 4))
        at_lo[0], at = place("attn_lo0", [P, KC, P], F32R, at)
        assert at <= r_ks
        at_raw[1], at = place("attn_rows1", [P, KC, P], F32, r_w)
        at_hi[1], at = place("attn_hi1", [P, KC, P], F32R, at)
        at_lo[1], at = place("attn_lo1", [P, KC, P], F32R, at)
        assert at <= r_w + NKV * QH * 4
        inv[1], at = place("inv_tile1", [P, KC, P], F32, r_ks)
        res[1], at = place("residual1", [P, H], F32, at)
        res[0], at = place("residual0", [P, H], F32, r_ks + NKV * NTE * 4)

        ps = stack.enter_context(nc.psum_tensor("ps", [P, 8, BANK], F32))

        q_scr = nc.dram_tensor("q_scratch", [2, B, HALVES, P, QH], F32, kind="Internal").ap()
        at_scr = nc.dram_tensor("attn_scratch", [P, KC, ROWS], F32, kind="Internal").ap()
        den_scr = nc.dram_tensor("den_scratch", [NH, ROWS], F32, kind="Internal").ap()
        inv_scr = nc.dram_tensor("inv_scratch", [NH, ROWS], F32, kind="Internal").ap()

        def sem(name):
            return stack.enter_context(nc.semaphore(name))

        zeroed = sem("zeroed")
        ident_set = sem("ident_set")
        ones_row = sem("ones_row")
        a_loaded = sem("a_loaded")
        b_loaded = sem("b_loaded")
        raw_in = [sem("raw_in0"), sem("raw_in1")]
        a_placed_pad = sem("a_pads")
        a_placed = sem("a_placed")
        a_turned = sem("a_turned")
        a_hi = sem("a_hi")
        a_lo = sem("a_lo")
        b_hi = sem("b_hi")
        b_lo = sem("b_lo")
        folded = sem("folded")
        w_summed = sem("w_summed")
        w_hi = sem("w_hi")
        w_lo = [sem("w_lo_dve"), sem("w_lo_pool")]
        x_loaded = [sem("x_loaded0"), sem("x_loaded1")]
        xt_turned = sem("xt_turned")
        xt_hi_set = sem("xt_hi_set")
        xt_lo_set = sem("xt_lo_set")
        q_done = sem("q_done")
        q_hi_set = sem("q_hi_set")
        q_lo_set = sem("q_lo_set")
        q_stored = [sem("q_stored0"), sem("q_stored1")]
        ctx_loaded = sem("ctx_loaded")
        ct_turned = sem("ct_turned")
        ct_hi_set = sem("ct_hi_set")
        ct_lo_set = sem("ct_lo_set")
        k_done = sem("k_done")
        k_hi_set = sem("k_hi_set")
        k_lo_set = sem("k_lo_set")
        v_done = sem("v_done")
        v_set = sem("v_set")
        q_in = [[sem(f"q_in{h}{par}") for par in range(2)] for h in range(HALVES)]
        nat_done = sem("nat_done")
        max_done = sem("max_done")
        m_turned = sem("m_turned")
        m_neg = sem("m_neg")
        m_in = [sem("m_in0"), sem("m_in1")]
        st_done = sem("st_done")
        exp_done = sem("exp_done")
        pv_done = sem("pv_done")
        psum_added = sem("prob_sums")
        den_done = sem("den_done")
        den_copied = sem("den_copied")
        den_stored = sem("den_stored")
        den_in = sem("den_in")
        inv_set = sem("inv_set")
        inv_stored = sem("inv_stored")
        attn_set = sem("attn_set")
        attn_stored = [sem("attn_stored0"), sem("attn_stored1")]
        at_in = [sem("at_in0"), sem("at_in1")]
        res_in = [sem("res_in0"), sem("res_in1")]
        inv_in = [sem("inv_in0"), sem("inv_in1")]
        at_normal = sem("at_normal")
        at_hi_set = sem("at_hi_set")
        at_lo_set = sem("at_lo_set")
        o_done = sem("o_done")
        o_added = sem("o_added")
        out_stored = [sem("out_stored0"), sem("out_stored1")]

        block = stack.enter_context(nc.Block())

        x_rows = x.rearrange("b q n -> (b q) n")
        out_rows = out.rearrange("b q n -> (b q) n")

        def ct_bank(b, k):
            return NAT + k % 2 if isinstance(b, int) and b == 0 else TURN

        def q_bank(g, c):
            first = isinstance(g, int) and g == 0 and c in (2, 3)
            return CTX + c % 2 if first else DENSE + c % 2

        def natural(w):
            return w.rearrange("(k p) n -> k p n", p=P)

        W_ALL = [
            (Wq, Aq, Bq, H), (Wk, Ak, Bk, KVW), (Wv, Av, Bv, KVW), (Wo, Ao, Bo, H),
        ]
        W_O = 3
        FIRST_BLOCK = [0, KC, KC + 2, KC + 4, 2 * KC + 4]
        QKV_BLOCKS = FIRST_BLOCK[W_O]

        A_LOADS = [16, 32, 48, 48 + 16 * NKV]
        B_LOADS = [16 * 4 * (w + 1) for w in range(4)]
        RAW_LOADS = []
        for g in range(FIRST_BLOCK[4]):
            before = RAW_LOADS[g - 2] if g >= 2 else 0
            RAW_LOADS.append(before + 16 * (JH if g >= QKV_BLOCKS else 1))

        def lo_by_pool(g):
            return int(g % 2 == 1 and not KC <= g < QKV_BLOCKS)

        def lo_count(g):
            return sum(lo_by_pool(n) == lo_by_pool(g) for n in range(g + 1))

        def wait_lo(eng, g):
            eng.wait_ge(w_lo[lo_by_pool(g)], lo_count(g))

        def wait_qkv(eng):
            wait_lo(eng, QKV_BLOCKS - 1)
            wait_lo(eng, KC - 1)

        def w_block(w, n):
            if w == 0:
                return wq_hi[:, n, :], wq_lo[:, n, :]
            if w == W_O:
                return wo_hi[:, n, :], wo_lo[:, n, :]
            hi, lo = (wk_hi, wk_lo) if w == 1 else (wv_hi, wv_lo)
            return (t[:, 4 * n:4 * n + 4, :].rearrange("p k n -> p (k n)") for t in (hi, lo))

        def run_steps(eng, step, wo_factors):
            full = ({"A", "D", "V", "T", "N", "Q", "E1"}, {"A", "D", "G", "T", "K", "C", "N", "Q"})
            step(-1, 0, (set(), {"K"}))
            step(-1, 1, ({"V", "T", "N", "E1"}, {"T", "K", "C", "N"}))
            wo_factors()
            step(0, 0, (full[0] - {"D"}, full[1] - {"G"}))
            with eng.Fori(0, (B - 4) // 2) as pair:
                step(pair, 1, full)
                step(pair, 2, full)
            step(B // 2 - 2, 1, (full[0], full[1] - {"C"}))
            step(B // 2 - 1, 0, ({"A", "D", "V", "N", "E1"}, {"A", "D", "G", "N", "W0"}))
            step(B // 2 - 1, 1, ({"A", "D", "W1"}, {"A", "D", "G", "W2"}))

        def store_den(eng, n, b, h):
            eng.wait_ge(den_copied, n + 1)
            rows = den_scr.rearrange("(j h r) n -> h j r n", j=JH, h=HALVES)
            eng.dma_start(rows[h, :, :, bass.ds(b * NQ, NQ)],
                          den_sb[0:P:HD, :].rearrange("j (r q) -> j r q", r=RH)).then_inc(den_stored, 16)

        def load_den(eng, b):
            eng.dma_start(den_rows[:, :], den_scr[:, bass.ds(b * NQ, NQ)]).then_inc(den_in, 16)

        def store_inv(eng, b):
            eng.wait_ge(inv_set, b + 1)
            eng.dma_start(inv_scr[:, bass.ds(b * NQ, NQ)], inv_rows[:, :]).then_inc(inv_stored, 16)

        def load_residual(eng, pair, par):
            if not isinstance(pair, int) or pair > 0:
                eng.wait_ge(out_stored[par], 16 * pair)
            eng.dma_start(res[par][:, :], x_rows[bass.ds((2 * pair + par) * P, P), :]).then_inc(res_in[par], 16)

        @block.sync
        def _(sp):
            def load_ab(w):
                W, A, Bm, width = W_ALL[w]
                if w:
                    sp.wait_ge(a_placed, w)
                if w == W_O:
                    heads = A.rearrange("(g r d) e -> g d r e", g=NKV, r=RH)
                    for g in range(NKV):
                        half, j = g // JH, g % JH
                        sp.dma_start(a_in[j * HD:(j + 1) * HD, half * RH:(half + 1) * RH, :], heads[g]
                                     ).then_inc(a_loaded, 16)
                else:
                    sp.dma_start(a_in[:, :, :], A.rearrange("(k p) r -> p k r", p=P)).then_inc(a_loaded, 16)
                if w:
                    sp.wait_ge(b_lo, w)
                else:
                    sp.wait_ge(zeroed, 1)
                for quad in range(4):
                    sp.dma_start(b_in[32 * quad:32 * quad + R, 0:width], Bm).then_inc(b_loaded, 16)

            def load_raw(w, n):
                W = W_ALL[w][0]
                g = FIRST_BLOCK[w] + n
                raw = raw2 if w == W_O else raw1
                if g >= 2:
                    sp.wait_ge(w_summed, g - 1)
                if w == W_O:
                    half, r = n // RH, n % RH
                    for j in range(JH):
                        row = ((half * JH + j) * RH + r) * HD
                        sp.dma_start(raw[g % 2][j * HD:(j + 1) * HD, :], W[row:row + HD, :]).then_inc(raw_in[g % 2], 16)
                elif w == 0:
                    sp.dma_start(raw[g % 2][:, :], W[n * P:(n + 1) * P, :]).then_inc(raw_in[g % 2], 16)
                else:
                    sp.dma_start(raw[g % 2][:, :].rearrange("p (k n) -> p k n", k=4),
                                 W[n * 4 * P:(n + 1) * 4 * P, :].rearrange("(k p) n -> p k n", p=P)
                                 ).then_inc(raw_in[g % 2], 16)

            def load_x(g):
                for half in range(2):
                    load_x_half(g, half)

            def load_x_half(g, half):
                cols = slice(half * H // 2, (half + 1) * H // 2)
                sp.dma_start(x_in[:, :, cols], x[bass.ds(g * QG, QG), :, cols].rearrange("b q n -> q b n")
                             ).then_inc(x_loaded[half], 16)

            def load_ctx(b):
                sp.dma_start(ctx_in[:, :, :],
                             ctxt[bass.ds(b, 1), :, :].rearrange("b (t p) n -> p (b t) n", p=TR)
                             ).then_inc(ctx_loaded, 16)

            load_ab(0)
            load_x_half(0, 0)
            load_raw(0, 0)
            load_raw(0, 1)
            load_x_half(0, 1)
            for n in range(2, KC):
                load_raw(0, n)
            load_ab(1)
            for n in range(2):
                load_raw(1, n)

            def store_q(g, n):
                half, r0 = n // 2, 2 * (n % 2)
                sp.wait_ge(q_lo_set, g * 2 * RH + 2 * (n + 1))
                for hl, t in ((0, qev_hi), (1, qev_lo)):
                    sp.dma_start(q_scr[hl, bass.ds(g * QG, QG), half, :, r0 * NQ:(r0 + 2) * NQ]
                                 .rearrange("b p n -> p b n"),
                                 t[:, :, r0:r0 + 2, :].bitcast(F32).rearrange("p b r q -> p b (r q)")
                                 ).then_inc(q_stored[n % 2], 16)

            def next_x(g):
                sp.wait_ge(xt_turned, (g + 1) * KC)
                load_x(g + 1)

            next_x(0)
            for n in range(QS // 2):
                store_q(0, n)
            load_ab(2)
            for n in range(2):
                load_raw(2, n)
            for n in range(QS // 2, QS):
                store_q(0, n)
            load_ctx(0)
            load_ab(W_O)
            with sp.Fori(1, GROUPS - 1) as g:
                next_x(g)
                for n in range(QS):
                    store_q(g, n)
            for n in range(QS):
                store_q(GROUPS - 1, n)

            def load_q(pair, off, h):
                b = 2 * pair + off
                for n, hl in enumerate((0, 1, 0)):
                    sp.dma_start(qst[off % 2][32 * n:32 * n + HD, h * JH:(h + 1) * JH, :].bitcast(F32),
                                 q_scr[hl, bass.ds(b, 1), h, :, :].rearrange("b (j d) n -> d (b j) n", d=HD)
                                 ).then_inc(q_in[h][off % 2], 16)

            sp.wait_ge(q_done, GROUPS * 2 * RH)
            load_q(0, 0, 0)
            sp.wait_ge(ct_turned, KC)
            load_ctx(1)
            load_q(0, 0, 1)
            load_q(0, 1, 0)
            load_q(0, 1, 1)
            for par in range(2):
                sp.wait_ge(q_stored[par], GROUPS * QS // 2 * 32)

            def store_attn(b, h):
                sp.wait_ge(attn_set, 2 * b + h + 1)
                sp.dma_start(at_scr[:, h * RH:(h + 1) * RH, bass.ds(b * NQ, NQ)], attn[h][:, :, :]
                             ).then_inc(attn_stored[h], 16)

            def load_inv(t, par):
                for j in range(JH):
                    sp.dma_start(inv[par][j * HD:(j + 1) * HD, :, :],
                                 inv_scr[j * KC:(j + 1) * KC, bass.ds(t * P, P)].partition_broadcast(HD)
                                 ).then_inc(inv_in[par], 16)

            def load_attn(pair, par):
                t = 2 * pair + par
                if isinstance(pair, int) and pair < 2:
                    for h in range(HALVES):
                        sp.wait_ge(attn_stored[h], 16 * 5)
                    sp.wait_ge(inv_stored, 16 * 5)
                if not isinstance(pair, int) or pair > 0:
                    sp.wait_ge(at_lo_set, t - 1)
                sp.dma_start(at_raw[par][:, :, :], at_scr[:, :, bass.ds(t * P, P)]).then_inc(at_in[par], 16)
                load_inv(t, par)

            def step(pair, off, has):
                b = 2 * pair + off
                for h in range(HALVES):
                    if "W0" in has[h]:
                        load_attn(0, 0)
                    if "W1" in has[h]:
                        sp.wait_ge(st_done, NS * 2 * (B - 1))
                        load_attn(0, 1)
                        load_residual(sp, 0, 1)
                    for kind, i, k in half_order(h, has[h]):
                        if kind == "A":
                            store_attn(b - 1 + h, 1 - h)
                        elif kind == "D":
                            store_den(sp, 2 * b + h - 1, b - 1 + h, 1 - h)
                            if "G" in has[h]:
                                load_den(sp, b - 1)
                        elif kind == "J":
                            store_inv(sp, b - 1)
                        elif kind == "K" and i == 1 and k == 0 and "C" in has[h]:
                            sp.wait_ge(ct_turned, (b + 3) * KC)
                            load_ctx(b + 3)
                        elif kind == "M":
                            sp.wait_ge(m_neg, 2 * (b + 1) + h + 1)
                            sp.dma_start(qst[(off + 1) % 2][STK:STM, h * JH:(h + 1) * JH, :].bitcast(F32)
                                         .rearrange("p j (r q) -> p (j r) q", r=RH),
                                         neg_max[:, h, :].bitcast(F32)).then_inc(m_in[h], 16)
                        elif kind == "W" and i + 1 in range(2, KC):
                            load_raw(W_O, i + 1)
                        elif kind == "Z" and (i, k) == (0, 0):
                            load_attn(1, 0)
                        elif kind == "E" and "Q" in has[h]:
                            sp.wait_ge(st_done, NS * (2 * b + h + 1))
                            load_q(pair, off + 2, h)

            def wo_factors():
                load_raw(W_O, 0)
                load_raw(W_O, 1)

            run_steps(sp, step, wo_factors)
            load_attn(1, 1)
            store_attn(B - 1, 1)
            sp.wait_ge(st_done, NS * 2 * B)
            load_residual(sp, 0, 0)
            for h in range(HALVES):
                sp.wait_ge(attn_stored[h], 16 * B)
            sp.wait_ge(inv_stored, 16 * (B - 1))
            with sp.Fori(2, OT // 2 - 1) as pair:
                for par in range(2):
                    load_attn(pair, par)
            load_attn(OT // 2 - 1, 0)
            sp.wait_ge(inv_stored, 16 * B)
            load_attn(OT // 2 - 1, 1)

        @block.gpsimd
        def _(pool):
            def pool_lo(w, n):
                g = FIRST_BLOCK[w] + n
                pool.wait_ge(w_hi, g + 1)
                hi, lo = w_block(w, n)
                pool.tensor_tensor(lo, (wsum2 if w == W_O else wsum1)[g % 2][:, :], hi, ALU.subtract
                                   ).then_inc(w_lo[1], 1)

            pool.memset(b_in[:, :], 0.0).then_inc(zeroed, 1)
            pool.memset(ident[:, :], 0.0).then_inc(ident_set, 1)
            pool.wait_ge(ident_set, 1)
            pool.affine_select(out=ident[:, :], in_=ident[:, :], compare_op=ALU.not_equal, fill=1.0, base=0,
                               pattern=[[-1, P]], channel_multiplier=1).then_inc(ident_set, 1)
            pool.memset(ones[:, :], 1.0).then_inc(ident_set, 1)
            for n in range(1, KC, 2):
                pool_lo(0, n)
            wait_qkv(pool)
            for par in range(2):
                pool.memset(kst[par][STK:STM, :, :].bitcast(F32), 1.0).then_inc(ones_row, 1)
                pool.wait_ge(ones_row, par + 1)
            pool.wait_ge(q_done, GROUPS * 2 * RH)
            for par, t in enumerate((ct_hi, ct_lo)):
                pool.memset(t[:, :, NT:NTE].bitcast(F32), 0.0).then_inc(ones_row, 1)
                pool.wait_ge(ones_row, par + 3)

            def step(pair, off, has):
                b = 2 * pair + off
                for h in range(HALVES):
                    n = 2 * b + h
                    for kind, i, k in half_order(h, has[h]):
                        if kind == "S" and i == 2 * JH - 1:
                            at_least(pool, den_done, n)
                            pool.wait_ge(exp_done, NS * n + 2 * JH)
                            pool.tensor_tensor(prob_sum[:, :, :], probs[:, 0, :, :], probs[:, 1, :, :], ALU.add
                                               ).then_inc(psum_added, 1)
                        elif kind == "S" and i == NS - 1:
                            pool.wait_ge(psum_added, 2 * n + 1)
                            pool.wait_ge(exp_done, NS * (n + 1))
                            pool.tensor_tensor(prob_sum[:, :, :], prob_sum[:, :, :], probs[:, 2, :, :], ALU.add
                                               ).then_inc(psum_added, 1)
                        elif kind == "W" and lo_by_pool(QKV_BLOCKS + i):
                            pool_lo(W_O, i)

            run_steps(pool, step, lambda: None)

        @block.tensor
        def _(pe):
            pe.wait_ge(ident_set, 3)

            def mm3(dst, l_hi, l_lo, r_hi, r_lo, start, stop):
                pe.matmul(dst, l_hi, r_hi, start=start, stop=False)
                pe.matmul(dst, l_hi, r_lo, start=False, stop=False)
                return pe.matmul(dst, l_lo, r_hi, start=False, stop=stop)

            def turn_a(w, bank):
                if w:
                    pe.wait_ge(w_summed, FIRST_BLOCK[w])
                pe.wait_ge(a_placed, w + 1)
                for k in range(KC):
                    mm = pe.transpose(ps[:, bank + k // 4, (k % 4) * P:(k % 4 + 1) * P],
                                      a_dup[:, k, :, :].rearrange("p a r -> p (a r)"), ident[:, :])
                mm.then_inc(a_turned, 1)

            def fold(w, n, bank):
                g = FIRST_BLOCK[w] + n
                width = W_ALL[w][3]
                a_st, b_st = (ast2, bst2) if w == W_O else (ast1, bst1)
                if n == 0:
                    pe.wait_ge(a_lo, w + 1)
                    pe.wait_ge(b_lo, w + 1)
                else:
                    pe.wait_ge(w_summed, g)
                for m in range(2):
                    if width == H:
                        mm = pe.matmul(ps[:, bank + m, :], a_st[:, n, :], b_st[:, m * BANK:(m + 1) * BANK],
                                       start=True, stop=True)
                    else:
                        for k in range(2):
                            mm = pe.matmul(ps[:, bank + m, k * KVW:(k + 1) * KVW], a_st[:, 4 * n + 2 * m + k, :],
                                           b_st[:, 0:KVW], start=True, stop=True)
                mm.then_inc(folded, 1)

            def turn_x(g, k):
                if k in (0, KC // 2):
                    pe.wait_ge(x_loaded[k // (KC // 2)], 16 * g + 16)
                at_least(pe, xt_lo_set, g * KC + k - 1)
                for b in range(QG):
                    mm = pe.transpose(ps[:, NAT + k % 2, b * NQ:(b + 1) * NQ], x_in[:, b, k * P:(k + 1) * P],
                                      ident[0:NQ, 0:NQ])
                mm.then_inc(xt_turned, 1)

            def q_piece(g, c, k):
                cols = slice(c * P, (c + 1) * P)
                return mm3(ps[:, q_bank(g, c), 0:QG * NQ], wq_hi[:, k, cols], wq_lo[:, k, cols],
                           xt_hi[:, k, :], xt_lo[:, k, :], k == 0, k == KC - 1)

            def q_chunk(g, c, after={}):
                if isinstance(g, int) and g == 0 and c in (4, 5):
                    pe.wait_ge(q_lo_set, c - 3)
                elif c >= 1:
                    pe.wait_ge(q_lo_set, g * 2 * RH + c - 1)
                for k in range(KC):
                    if c == 0:
                        pe.wait_ge(xt_lo_set, g * KC + k + 1)
                    mm = q_piece(g, c, k)
                    if c == 2 * RH - 1:
                        if k == KC - 1:
                            mm.then_inc(q_done, 1)
                        if isinstance(g, int) and g == GROUPS - 1:
                            turn_ctx(0, k)
                        else:
                            turn_x(g + 1, k)
                    if k in after:
                        after[k]()
                if c < 2 * RH - 1:
                    mm.then_inc(q_done, 1)

            def turn_ctx(b, k):
                if k == 0:
                    pe.wait_ge(ctx_loaded, 16 * (b + 1))
                bank = ct_bank(b, k)
                if bank != TURN:
                    at_least(pe, ct_lo_set, k - 1)
                elif k == 0:
                    pe.wait_ge(k_lo_set, NKV * b)
                else:
                    pe.wait_ge(ct_lo_set, b * KC + k)
                for t in range(TC):
                    mm = pe.transpose(ps[:, bank, t * TR:(t + 1) * TR], ctx_in[:, t, k * P:(k + 1) * P],
                                      ident[0:TR, 0:TR])
                mm.then_inc(ct_turned, 1)

            def q_first(k):
                wait_lo(pe, k)
                pe.wait_ge(xt_lo_set, k + 1)
                for c in range(4):
                    mm = q_piece(0, c, k)
                    if k == KC - 1:
                        mm.then_inc(q_done, 1)

            turn_a(0, FOLD)
            for k in range(KC):
                turn_x(0, k)
                fold(0, k, FOLD)
                if k >= 2:
                    q_first(k - 2)
            q_first(KC - 2)
            q_first(KC - 1)
            turn_a(1, FOLD)
            q_chunk(0, 4)
            fold(1, 0, FOLD)
            q_chunk(0, 5, {4: lambda: fold(1, 1, FOLD)})
            q_chunk(0, 6, {4: lambda: turn_a(2, FOLD)})
            q_chunk(0, 7, {0: lambda: fold(2, 0, FOLD), 5: lambda: fold(2, 1, FOLD)})
            pe.wait_ge(q_lo_set, 2 * RH - 1)
            with pe.Fori(1, GROUPS - 1) as g:
                for c in range(2 * RH):
                    q_chunk(g, c)
                pe.wait_ge(q_lo_set, g * 2 * RH + 2 * RH - 1)
            for c in range(2 * RH):
                q_chunk(GROUPS - 1, c)
            pe.wait_ge(q_lo_set, GROUPS * 2 * RH - 1)
            wait_qkv(pe)
            pe.wait_ge(ones_row, 4)

            def step(pair, off, has):
                b = 2 * pair + off
                cur, nxt = off % 2, (off + 1) % 2
                for h in range(HALVES):
                    n = 2 * b + h
                    m = 2 * (b + 1) + h
                    for kind, i, k in half_order(h, has[h]):
                        if kind == "V":
                            if k == 0 and i == 0:
                                at_least(pe, k_lo_set, NKV * (b + 1) + JH)
                            dst = ps[0:TR, VA + i // 2, (i % 2) * KVW:(i % 2 + 1) * KVW]
                            rows = slice(i * TR, (i + 1) * TR)
                            pe.matmul(dst, ct_hi[:, k, rows], wv_hi[:, k, :], start=(k == 0 and i != 1), stop=False,
                                      skip_group_check=True)
                            pe.matmul(dst, ct_hi[:, k, rows], wv_lo[:, k, :], start=False, stop=False,
                                      skip_group_check=True)
                            mm = pe.matmul(dst, ct_lo[:, k, rows], wv_hi[:, k, :], start=False,
                                           stop=(k == KC - 1), skip_group_check=True)
                            if k == KC - 1 and i >= 1:
                                mm.then_inc(v_done, 1)
                        elif kind == "T":
                            turn_ctx(b + 2, i)
                        elif kind == "K":
                            if k == 0:
                                at_least(pe, v_set, 2 * (b + 1) + 2)
                                if i == 1:
                                    pe.wait_ge(ct_lo_set, (b + 3) * KC)
                            if i == 0:
                                pe.wait_ge(ct_lo_set, (b + 2) * KC + k + 1)
                            cols = slice(i * P, (i + 1) * P)
                            mm = mm3(ps[:, (VA, TURN)[i], 0:NTE], wk_hi[:, k, cols], wk_lo[:, k, cols],
                                     ct_hi[:, k, :], ct_lo[:, k, :], k == 0, k == KC - 1)
                            if k == KC - 1:
                                mm.then_inc(k_done, 1)
                        elif kind == "S":
                            if i == 0:
                                pe.wait_ge(m_in[h], 16 * (b + 1))
                            same = [s for s in range(i) if score_bank(s) == score_bank(i)]
                            if i == 0:
                                at_least(pe, exp_done, NS * n - 1)
                            elif i == S_IN_DEN[0]:
                                at_least(pe, den_copied, n)
                            else:
                                pe.wait_ge(exp_done, NS * n + same[-1] + 1)
                            if i == S_IN_DEN[0] and isinstance(n, int) and n == 0:
                                pe.wait_ge(a_lo, W_O + 1)
                            g, c = h * JH + i % JH, i // JH
                            pe.matmul(ps[0:TR, score_bank(i), 0:QH], kst[cur][0:STM, g, c * TR:(c + 1) * TR],
                                      qst[cur][0:STM, g, :], start=True, stop=True).then_inc(st_done, 1)
                        elif kind == "N":
                            if i == 0:
                                pe.wait_ge(q_in[h][nxt], 48 * (pair + (off + 1) // 2 + 1))
                                pe.wait_ge(k_lo_set, JH * (m + 1))
                                at_least(pe, m_neg, m)
                            at_least(pe, max_done, NN * m + i - 1)
                            g, rr = h * JH + i // RH, i % RH
                            mm = pe.matmul(ps[0:NQ, NAT + i % 2, 0:NTE], qst[nxt][0:STK, g, rr * NQ:(rr + 1) * NQ],
                                           kst[nxt][0:STK, g, :], start=True, stop=True)
                            mm.then_inc(nat_done, 1)
                        elif kind == "M":
                            pe.wait_ge(max_done, NN * (m + 1))
                            pe.transpose(ps[0:JH * RH, NAT, 0:NQ], maxima[:, h, :], ident[0:NQ, 0:NQ]
                                         ).then_inc(m_turned, 1)
                        elif kind == "P":
                            pe.wait_ge(exp_done, NS * n + JH * (i + 1))
                            if i == 0:
                                at_least(pe, attn_set, n)
                                pe.wait_ge(v_set, 2 * (b + 1))
                            for j in range(JH):
                                g = h * JH + j
                                mm = pe.matmul(ps[HD * j:HD * (j + 1), CTX, 0:QH],
                                               v_sb[cur][:, i, g * HD:(g + 1) * HD], probs[:, i, j, :],
                                               start=(i == 0), stop=(i == TC - 1))
                            mm.then_inc(pv_done, 1)
                        elif kind == "D":
                            denominators(n - 1)
                        elif kind == "W":
                            if i == 0:
                                pe.wait_ge(v_set, 2 * B)
                            fold(W_O, i, FOLD_O)
                        elif kind == "O":
                            if i == 0:
                                pe.wait_ge(at_lo_set, 1)
                                pe.wait_ge(m_neg, 2 * B)
                            wait_lo(pe, QKV_BLOCKS + i)
                            for m in range(2):
                                o_piece(0, m, i, NAT).then_inc(o_done, 1) if i == KC - 1 else o_piece(0, m, i, NAT)

                        elif kind == "Z":
                            if i == 0 and k == 0:
                                pe.wait_ge(at_lo_set, 2)
                                pe.wait_ge(w_summed, FIRST_BLOCK[4])
                            mm = o_piece(1, i, k, OUT[1])
                            if k == KC - 1:
                                mm.then_inc(o_done, 1)

            def o_piece(par, m, k, bank):
                cols = slice(m * BANK, (m + 1) * BANK)
                return mm3(ps[:, bank + m, :], at_hi[par][:, k, :], at_lo[par][:, k, :],
                           wo_hi[:, k, cols], wo_lo[:, k, cols], k == 0, k == KC - 1)

            def denominators(n):
                pe.wait_ge(psum_added, 2 * n + 2)
                for j in range(JH):
                    mm = pe.matmul(ps[HD * j:HD * (j + 1), DEN, 0:QH], ones[:, :], prob_sum[:, j, :],
                                   start=True, stop=True)
                mm.then_inc(den_done, 1)

            def wo_factors():
                turn_a(W_O, CTX)

            run_steps(pe, step, wo_factors)
            denominators(2 * B - 1)

            def tile(pair, par):
                t = 2 * pair + par
                pe.wait_ge(at_lo_set, t + 1)
                for m in range(2):
                    if isinstance(pair, int) and par == 0:
                        pe.wait_ge(attn_set, 2 * B)
                        pe.wait_ge(den_copied, 2 * B)
                    else:
                        pe.wait_ge(o_added, 2 * t + m - 3)
                    for k in range(KC):
                        mm = o_piece(par, m, k, OUT[par])
                    mm.then_inc(o_done, 1)

            tile(1, 0)
            tile(1, 1)
            with pe.Fori(2, OT // 2) as pair:
                tile(pair, 0)
                tile(pair, 1)

        @block.scalar
        def _(act):
            def ab_hi(w, bank):
                a_st, b_st = (ast2, bst2) if w == W_O else (ast1, bst1)
                width = W_ALL[w][3]
                act.wait_ge(b_loaded, B_LOADS[w])
                at_least(act, folded, FIRST_BLOCK[w])
                act.activation(b_st[:, 0:width], b_in[:, 0:width], ACT.Copy).then_inc(b_hi, 1)
                act.wait_ge(a_turned, w + 1)
                act.activation(a_st[:, :, :].rearrange("p k n -> p (k n)"),
                               ps[:, bank:bank + 2, :].rearrange("p a n -> p (a n)"), ACT.Copy, scale=LORA
                               ).then_inc(a_hi, 1)

            def block_hi(w, n):
                g = FIRST_BLOCK[w] + n
                act.wait_ge(w_summed, g + 1)
                hi, lo = w_block(w, n)
                act.activation(hi, (wsum2 if w == W_O else wsum1)[g % 2][:, :], ACT.Copy).then_inc(w_hi, 1)

            def x_hi(g, k):
                act.wait_ge(xt_turned, g * KC + k + 1)
                act.activation(xt_hi[:, k, :], ps[:, NAT + k % 2, 0:QG * NQ], ACT.Copy).then_inc(xt_hi_set, 1)

            def q_hi(g, c):
                if c % 2 == 0:
                    at_least(act, q_stored[c // 2 % 2], 32 * (QS // 2 * g + c // 4))
                act.wait_ge(q_done, g * 2 * RH + c + 1)
                act.activation(qev_hi[:, :, c % RH, :],
                               ps[:, q_bank(g, c), 0:QG * NQ].rearrange("p (b q) -> p b q", b=QG), ACT.Copy
                               ).then_inc(q_hi_set, 1)

            def ctx_hi(b, k):
                act.wait_ge(ct_turned, b * KC + k + 1)
                act.activation(ct_hi[:, k, 0:NT], ps[:, ct_bank(b, k), 0:NT], ACT.Copy).then_inc(ct_hi_set, 1)

            def k_hi(b, par, half, j):
                act.wait_ge(k_done, 2 * b + half + 1)
                at_least(act, st_done, NS * (2 * (b - 2) + half + 1))
                for quad in range(2):
                    op = act.activation(kst[par][HD * quad:HD * (quad + 1), half * JH + j, :],
                                        ps[HD * j:HD * (j + 1), (VA, TURN)[half], 0:NTE], ACT.Copy)
                op.then_inc(k_hi_set, 1)

            ab_hi(0, FOLD)
            for k in range(KC):
                x_hi(0, k)
                block_hi(0, k)
            q_hi(0, 0)
            q_hi(0, 1)
            ab_hi(1, FOLD)
            for c in range(2, 5):
                q_hi(0, c)
            block_hi(1, 0)
            block_hi(1, 1)
            q_hi(0, 5)
            ab_hi(2, FOLD)
            q_hi(0, 6)
            for k in range(KC):
                x_hi(1, k)
                if k in (0, 5):
                    block_hi(2, k // 5)
            q_hi(0, 7)
            with act.Fori(1, GROUPS - 1) as g:
                for c in range(2 * RH - 1):
                    q_hi(g, c)
                for k in range(KC):
                    x_hi(g + 1, k)
                q_hi(g, 2 * RH - 1)
            for c in range(2 * RH - 1):
                q_hi(GROUPS - 1, c)
            for k in range(KC):
                ctx_hi(0, k)
            q_hi(GROUPS - 1, 2 * RH - 1)

            def step(pair, off, has):
                b = 2 * pair + off
                cur, nxt = off % 2, (off + 1) % 2
                for h in range(HALVES):
                    n = 2 * b + h
                    m = 2 * (b + 1) + h
                    for kind, i, k in half_order(h, has[h]):
                        if kind == "V" and k == KC - 1 and i >= 1:
                            act.wait_ge(v_done, 2 * (b + 1) + i)
                            wide = 2 * KVW if i == 1 else KVW
                            c0 = 0 if i == 1 else 2
                            act.activation(v_sb[nxt][:, c0:i + 1, :].rearrange("p c n -> p (c n)"),
                                           ps[0:TR, VA + i // 2, 0:wide], ACT.Copy).then_inc(v_set, 1)
                        elif kind == "T":
                            ctx_hi(b + 2, i)
                        elif kind == "E0":
                            k_hi(b + 2, cur, 0, i)
                        elif kind == "E1":
                            k_hi(b + 1, nxt, 1, i)
                        elif kind == "S":
                            c, j = i // JH, i % JH
                            act.wait_ge(st_done, NS * n + i + 1)
                            at_least(act, pv_done, 3 * n + c - 2)
                            at_least(act, psum_added, 2 * n - (1 if c < 2 else 0))
                            act.activation(probs[:, c, j, :], ps[0:TR, score_bank(i), 0:QH], ACT.Exp, scale=SM
                                           ).then_inc(exp_done, 1)
                        elif kind == "D":
                            copy_den(n - 1)
                        elif kind == "M":
                            act.wait_ge(m_turned, m + 1)
                            at_least(act, m_in[h], 16 * (b + 1))
                            act.activation(neg_max[:, h, :], ps[0:JH * RH, NAT, 0:NQ], ACT.Copy, scale=-1.0
                                           ).then_inc(m_neg, 1)
                        elif kind == "W":
                            block_hi(W_O, i)
                            if i == OLAG - 1:
                                split(0, 0)
                        elif kind == "O" and i == 3:
                            split(0, 1)
                        elif kind == "Z" and (i, k) == (1, 0):
                            split(1, 0)

            def copy_den(n):
                act.wait_ge(den_done, n + 1)
                at_least(act, den_stored, 16 * n)
                act.activation(den_sb[:, :], ps[:, DEN, 0:QH], ACT.Copy).then_inc(den_copied, 1)

            def split(pair, par):
                t = 2 * pair + par
                act.wait_ge(at_normal, t + 1)
                at_least(act, o_done, 2 * (t - 1))
                act.activation(at_hi[par][:, :, :], at_raw[par][:, :, :], ACT.Copy).then_inc(at_hi_set, 1)

            def store_tile(pair, par):
                t = 2 * pair + par
                act.wait_ge(o_added, 2 * t + 2)
                act.dma_start(out_rows[bass.ds(t * P, P), :], res[par][:, :]).then_inc(out_stored[par], 16)

            def wo_factors():
                for par in range(2):
                    act.wait_ge(q_stored[par], GROUPS * QS // 2 * 32)
                ab_hi(W_O, CTX)

            run_steps(act, step, wo_factors)
            copy_den(2 * B - 1)
            store_den(act, 2 * B - 1, B - 1, 1)
            split(1, 1)
            for par in range(2):
                store_tile(0, par)
                load_residual(act, 1, par)
            act.wait_ge(den_stored, 16 * 2 * B)
            act.wait_ge(inv_set, B - 1)
            load_den(act, B - 1)
            store_inv(act, B - 1)
            with act.Fori(2, OT // 2) as pair:
                for par in range(2):
                    split(pair, par)
                    store_tile(pair - 1, par)
                    load_residual(act, pair, par)
            for par in range(2):
                store_tile(OT // 2 - 1, par)
            for par in range(2):
                act.wait_ge(out_stored[par], 16 * (OT // 2))

        @block.vector
        def _(dve):
            dve.memset(a_dup[:, :, :, :].rearrange("p k a r -> p (k a r)"), 0.0).then_inc(a_placed_pad, 1)
            dve.wait_ge(a_placed_pad, 1)

            def ab_place(w):
                dve.wait_ge(a_loaded, A_LOADS[w])
                at_least(dve, a_turned, w)
                for quad in range(4):
                    op = dve.tensor_copy(a_dup[:, :, quad, 0:R], a_in[:, :, :])
                op.then_inc(a_placed, 1)

            def ab_lo(w, bank):
                a_st, b_st = (ast2, bst2) if w == W_O else (ast1, bst1)
                width = W_ALL[w][3]
                dve.wait_ge(b_hi, w + 1)
                for quad in (1, 3):
                    rows = slice(32 * quad, 32 * quad + 32)
                    op = dve.tensor_tensor(b_st[rows, 0:width], b_in[rows, 0:width], b_st[rows, 0:width], ALU.subtract)
                op.then_inc(b_lo, 1)
                dve.wait_ge(a_hi, w + 1)
                rows = slice(2 * 32, 4 * 32)
                st = a_st[rows, :, :].rearrange("p k n -> p (k n)")
                dve.scalar_tensor_tensor(out=st, in0=ps[rows, bank:bank + 2, :].rearrange("p a n -> p (a n)"),
                                         scalar=LORA, in1=st, op0=ALU.mult, op1=ALU.subtract).then_inc(a_lo, 1)

            def block_sum(w, n, bank):
                g = FIRST_BLOCK[w] + n
                raw, wsum = (raw2, wsum2) if w == W_O else (raw1, wsum1)
                dve.wait_ge(folded, g + 1)
                dve.wait_ge(raw_in[g % 2], RAW_LOADS[g])
                if g >= 2:
                    wait_lo(dve, g - 2)
                if w == 0:
                    for m in range(2):
                        cols = slice(m * BANK, (m + 1) * BANK)
                        op = dve.tensor_tensor(
                            wsum[g % 2][:, cols].rearrange("p (r j d) -> p j r d", r=RH, j=JH),
                            ps[:, bank + m, :].rearrange("p (j r d) -> p j r d", j=JH, r=RH),
                            raw[g % 2][:, cols].rearrange("p (j r d) -> p j r d", j=JH, r=RH), ALU.add)
                else:
                    op = dve.tensor_tensor(wsum[g % 2][:, :], ps[:, bank:bank + 2, :].rearrange("p a n -> p (a n)"),
                                           raw[g % 2][:, :], ALU.add)
                op.then_inc(w_summed, 1)

            def block_lo(w, n):
                g = FIRST_BLOCK[w] + n
                if lo_by_pool(g):
                    return
                dve.wait_ge(w_hi, g + 1)
                hi, lo = w_block(w, n)
                dve.tensor_tensor(lo, (wsum2 if w == W_O else wsum1)[g % 2][:, :], hi, ALU.subtract
                                  ).then_inc(w_lo[0], 1)

            def x_lo(g, k):
                dve.wait_ge(xt_hi_set, g * KC + k + 1)
                dve.tensor_tensor(xt_lo[:, k, :], ps[:, NAT + k % 2, 0:QG * NQ], xt_hi[:, k, :], ALU.subtract
                                  ).then_inc(xt_lo_set, 1)

            def q_lo(g, c):
                dve.wait_ge(q_hi_set, g * 2 * RH + c + 1)
                dve.tensor_tensor(qev_lo[:, :, c % RH, :],
                                  ps[:, q_bank(g, c), 0:QG * NQ].rearrange("p (b q) -> p b q", b=QG),
                                  qev_hi[:, :, c % RH, :], ALU.subtract).then_inc(q_lo_set, 1)

            def ctx_lo(b, k):
                dve.wait_ge(ct_hi_set, b * KC + k + 1)
                dve.tensor_tensor(ct_lo[:, k, 0:NT], ps[:, ct_bank(b, k), 0:NT], ct_hi[:, k, 0:NT], ALU.subtract
                                  ).then_inc(ct_lo_set, 1)

            def k_lo(b, par, half, j):
                dve.wait_ge(k_hi_set, NKV * b + half * JH + j + 1)
                dve.tensor_tensor(kst[par][2 * HD:3 * HD, half * JH + j, :],
                                  ps[HD * j:HD * (j + 1), (VA, TURN)[half], 0:NTE],
                                  kst[par][0:HD, half * JH + j, :], ALU.subtract).then_inc(k_lo_set, 1)

            ab_place(0)
            ab_lo(0, FOLD)
            for k in range(KC):
                x_lo(0, k)
                block_sum(0, k, FOLD)
                if k:
                    block_lo(0, k - 1)
            block_lo(0, KC - 1)
            ab_place(1)
            q_lo(0, 0)
            q_lo(0, 1)
            ab_lo(1, FOLD)
            for c in range(2, 5):
                q_lo(0, c)
            for n in range(2):
                block_sum(1, n, FOLD)
                block_lo(1, n)
            ab_place(2)
            q_lo(0, 5)
            ab_lo(2, FOLD)
            q_lo(0, 6)
            for k in range(KC):
                x_lo(1, k)
                if k in (0, 5):
                    block_sum(2, k // 5, FOLD)
                if k in (1, 6):
                    block_lo(2, k // 5)
            q_lo(0, 7)
            with dve.Fori(1, GROUPS - 1) as g:
                for c in range(2 * RH - 1):
                    q_lo(g, c)
                for k in range(KC):
                    x_lo(g + 1, k)
                q_lo(g, 2 * RH - 1)
            for c in range(2 * RH - 1):
                q_lo(GROUPS - 1, c)
            for k in range(KC):
                ctx_lo(0, k)
            q_lo(GROUPS - 1, 2 * RH - 1)
            ab_place(W_O)

            def invert(b):
                dve.wait_ge(den_in, 16 * (b + 1))
                at_least(dve, inv_stored, 16 * b)
                dve.reciprocal(inv_rows[:, :], den_rows[:, :]).then_inc(inv_set, 1)

            def copy_attn(b, n, h):
                dve.wait_ge(pv_done, TC * (n + 1))
                at_least(dve, attn_stored[h], 16 * b)
                dve.tensor_copy(attn[h][:, :, :].rearrange("p r q -> p (r q)"), ps[:, CTX, 0:QH]
                                ).then_inc(attn_set, 1)

            def step(pair, off, has):
                b = 2 * pair + off
                cur = off % 2
                for h in range(HALVES):
                    n = 2 * b + h
                    m = 2 * (b + 1) + h
                    for kind, i, k in half_order(h, has[h]):
                        if kind == "T":
                            ctx_lo(b + 2, i)
                        elif kind == "F0":
                            k_lo(b + 2, cur, 0, i)
                        elif kind == "F1":
                            k_lo(b + 1, (off + 1) % 2, 1, i)
                        elif kind == "N":
                            dve.wait_ge(nat_done, NN * m + i + 1)
                            dve.tensor_reduce(maxima[:, h, i:i + 1], ps[0:NQ, NAT + i % 2, 0:NT], AX.X,
                                              ALU.max).then_inc(max_done, 1)
                        elif kind == "I":
                            invert(b - 1)
                        elif kind == "A":
                            copy_attn(b - 1 + h, n - 1, 1 - h)
                        elif kind == "W":
                            block_sum(W_O, i, FOLD_O)
                            if i % 2 == 1:
                                block_lo(W_O, i - 1)
                            if i == OLAG - 1:
                                normalise(0, 0)
                                split(0, 0)
                        elif kind == "O" and i == 3:
                            normalise(0, 1)
                            split(0, 1)
                        elif kind == "Z" and (i, k) == (1, 0):
                            normalise(1, 0)
                            split(1, 0)

            def normalise(pair, par):
                dve.wait_ge(at_in[par], 16 * (pair + 1))
                dve.wait_ge(inv_in[par], 16 * JH * (pair + 1))
                dve.tensor_tensor(at_raw[par][:, :, :], at_raw[par][:, :, :], inv[par][:, :, :], ALU.mult
                                  ).then_inc(at_normal, 1)

            def split(pair, par):
                dve.wait_ge(at_hi_set, 2 * pair + par + 1)
                dve.tensor_tensor(at_lo[par][:, :, :], at_raw[par][:, :, :], at_hi[par][:, :, :], ALU.subtract
                                  ).then_inc(at_lo_set, 1)

            def add_residual(pair, par):
                t = 2 * pair + par
                dve.wait_ge(res_in[par], 16 * (pair + 1))
                for m in range(2):
                    dve.wait_ge(o_done, 2 * t + m + 1)
                    part = res[par][:, m * BANK:(m + 1) * BANK]
                    bank = NAT if isinstance(pair, int) and t == 0 else OUT[par]
                    dve.tensor_tensor(part, ps[:, bank + m, :], part, ALU.add).then_inc(o_added, 1)

            def wo_factors():
                ab_lo(W_O, CTX)

            run_steps(dve, step, wo_factors)
            copy_attn(B - 1, 2 * B - 1, 1)
            add_residual(0, 0)
            normalise(1, 1)
            add_residual(0, 1)
            split(1, 1)
            invert(B - 1)
            with dve.Fori(1, OT // 2 - 1) as pair:
                for par in range(2):
                    normalise(pair + 1, par)
                    add_residual(pair, par)
                    split(pair + 1, par)
            for par in range(2):
                add_residual(OT // 2 - 1, par)


_INS = ['x', 'ctx_4096', 'L0_xattn_Wq', 'L0_xattn_Aq', 'L0_xattn_Bq', 'L0_xattn_Wk', 'L0_xattn_Ak', 'L0_xattn_Bk',
        'L0_xattn_Wv', 'L0_xattn_Av', 'L0_xattn_Bv', 'L0_xattn_Wo', 'L0_xattn_Ao', 'L0_xattn_Bo']
_OUTS = [((B, NQ, H), 'float32')]


def kernel(**inputs):
    import numpy as _np
    import concourse.bacc as _bacc
    from concourse import mybir as _mybir
    from concourse.bass_utils import run_bass_kernel_spmd as _run

    nc = _bacc.Bacc("TRN2", target_bir_lowering=False, num_devices=1)
    arrays, args = {}, []
    for name in _INS:
        a = _np.ascontiguousarray(inputs[name])
        arrays[f"in_{name}_dram"] = a
        args.append(nc.dram_tensor(f"in_{name}_dram", a.shape, _mybir.dt.from_np(a.dtype), kind="ExternalInput").ap())
    for i, (shape, dtype) in enumerate(_OUTS):
        dt = _mybir.dt.from_np(_np.dtype(dtype))
        args.append(nc.dram_tensor(f"out_{i}_dram", shape, dt, kind="ExternalOutput").ap())
    xattn_kernel(nc, *args)
    r = _run(nc, [arrays], core_ids=[0])
    return r.results[0]["out_0_dram"]
```
